# Optimizing a Trainium2 kernel written in Bass

```python
import numpy as np
import jax
import jax.numpy as jnp

def _softmax(x, axis=-1):
    return jax.nn.softmax(x, axis=axis)

def _gelu(x):
    return jax.nn.gelu(x, approximate=True)

def _silu(x):
    return jax.nn.silu(x)

def _sigmoid(x):
    return jax.nn.sigmoid(x)

def _layernorm(x, axis=-1, eps=1e-05):
    m = jnp.mean(x, axis=axis, keepdims=True)
    v = jnp.var(x, axis=axis, keepdims=True)
    return (x - m) / jnp.sqrt(v + eps)

def _scatter_add(tgt, idx, src, axis=0):
    return tgt.at[idx].add(src)

def _segment_sum(src, seg, n):
    return jax.ops.segment_sum(src, seg, n)
kernel_name = 'mk_xattn_seq_d1_seqx_r2_d6ad87'

def setup_inputs(seed: int=0):
    np.random.seed(seed)
    _w = jnp.asarray

    def _rec_inputs():
        import jax
        import jax.numpy as jnp
        _rk = jax.random.key(seed)
        x = -0.000719 + 1.001 * jax.random.normal(jax.random.fold_in(_rk, 1), (4, 2048, 640), jnp.float32)
        _lenS = 2048 - jax.random.randint(jax.random.fold_in(_rk, 7), (4,), 0, max(1, 2048 // 4) + 1, jnp.int32)
        _lenS2 = 77 - jax.random.randint(jax.random.fold_in(_rk, 8), (4,), 0, max(1, 77 // 4) + 1, jnp.int32)
        _ctx_2048P = jax.random.normal(jax.random.fold_in(_rk, 11), (4, 16, 1024), jnp.float32)
        _ctx_2048c = jax.random.dirichlet(jax.random.fold_in(_rk, 511), 0.3 * jnp.ones((16,), jnp.float32), (4, 77))
        _ctx_2048t = jnp.einsum('bsk,bkd->bsd', _ctx_2048c, _ctx_2048P)
        _ctx_2048t = _ctx_2048t * jax.lax.rsqrt(jnp.mean(jnp.square(_ctx_2048t)) + 1e-12) * 0.953939
        ctx_2048 = 0.00257118 + 0.99863 * (_ctx_2048t + 0.3 * jax.random.normal(jax.random.fold_in(_rk, 611), (4, 77, 1024), jnp.float32))
        fside_S_0 = jax.random.uniform(jax.random.fold_in(_rk, 12), (2048,), jnp.float32, 0.0, 0.999706)
        return (x, ctx_2048, fside_S_0)
    x, ctx_2048, fside_S_0 = _rec_inputs()

    def _L0_xattn_setup():
        import jax, jax.numpy as jnp
        import numpy as np
        HEADS = 20
        NUM_TOKENS = 4
        IP_SCALE = 1.0
        SEM_SCALE = 0.5
        RESCALE = 1.0
        EPS = 1e-12

        def _l2norm(x, axis=-1):
            n = jnp.sqrt(jnp.sum(x * x, axis=axis, keepdims=True))
            return x / jnp.maximum(n, EPS)
        key = jax.random.key(seed)
        ks = jax.random.split(key, 10)
        B, S, C = (2, 512, 640)
        T, E = (81, 1024)
        inp = {'hidden_states': jax.random.normal(ks[0], (B, S, C), jnp.float32), 'encoder_hidden_states': jax.random.normal(ks[1], (B, T, E), jnp.float32), 'spatial_mask': jax.random.uniform(ks[2], (S,), jnp.float32), 'W_q': jax.random.normal(ks[3], (C, C), jnp.float32) * C ** (-0.5), 'W_k': jax.random.normal(ks[4], (E, C), jnp.float32) * E ** (-0.5), 'W_v': jax.random.normal(ks[5], (E, C), jnp.float32) * E ** (-0.5), 'W_k_ip': jax.random.normal(ks[6], (E, C), jnp.float32) * E ** (-0.5), 'W_v_ip': jax.random.normal(ks[7], (E, C), jnp.float32) * E ** (-0.5), 'W_out': jax.random.normal(ks[8], (C, C), jnp.float32) * C ** (-0.5), 'b_out': jnp.zeros((C,), jnp.float32)}
        return inp
    _L0_xattn_all = _L0_xattn_setup()
    _L0_xattn_in = {k: v for k, v in _L0_xattn_all.items() if k in ('W_q', 'W_k', 'W_v', 'W_k_ip', 'W_v_ip', 'W_out', 'b_out')}
    del _L0_xattn_all
    return {'x': x, 'ctx_2048': ctx_2048, 'fside_S_0': fside_S_0, 'L0_xattn_W_q': _L0_xattn_in['W_q'], 'L0_xattn_W_k': _L0_xattn_in['W_k'], 'L0_xattn_W_v': _L0_xattn_in['W_v'], 'L0_xattn_W_k_ip': _L0_xattn_in['W_k_ip'], 'L0_xattn_W_v_ip': _L0_xattn_in['W_v_ip'], 'L0_xattn_W_out': _L0_xattn_in['W_out'], 'L0_xattn_b_out': _L0_xattn_in['b_out']}

def reference(x, ctx_2048, fside_S_0, L0_xattn_W_q, L0_xattn_W_k, L0_xattn_W_v, L0_xattn_W_k_ip, L0_xattn_W_v_ip, L0_xattn_W_out, L0_xattn_b_out):
    import jax
    import jax.numpy as jnp

    def _L0_xattn_ref(hidden_states, encoder_hidden_states, spatial_mask, W_q, W_k, W_v, W_k_ip, W_v_ip, W_out, b_out):
        import jax, jax.numpy as jnp
        import numpy as np
        HEADS = 20
        NUM_TOKENS = 4
        IP_SCALE = 1.0
        SEM_SCALE = 0.5
        RESCALE = 1.0
        EPS = 1e-12

        def _l2norm(x, axis=-1):
            n = jnp.sqrt(jnp.sum(x * x, axis=axis, keepdims=True))
            return x / jnp.maximum(n, EPS)
        B, S, C = hidden_states.shape
        H = HEADS
        Dh = C // H
        attn_scale = Dh ** (-0.5)
        residual = hidden_states
        text_ehs = encoder_hidden_states[:, :-NUM_TOKENS]
        ip_ehs = encoder_hidden_states[:, -NUM_TOKENS:]

        def heads(x):
            return x.reshape(B, -1, H, Dh).transpose(0, 2, 1, 3)
        q = heads(hidden_states @ W_q)
        k_t = heads(text_ehs @ W_k)
        v_t = heads(text_ehs @ W_v)
        scores_t = jnp.einsum('bhsd,bhtd->bhst', q, k_t) * attn_scale
        probs_t = jax.nn.softmax(scores_t, axis=-1)
        text_out = jnp.einsum('bhst,bhtd->bhsd', probs_t, v_t)
        text_out = text_out.transpose(0, 2, 1, 3).reshape(B, S, C)
        k_ip = heads(ip_ehs @ W_k_ip)
        v_ip = heads(ip_ehs @ W_v_ip)
        attn_scores = jnp.einsum('bhsd,bhnd->bhsn', q, k_ip) * attn_scale
        qsem = jnp.einsum('bhst,bte->bhse', probs_t, text_ehs)
        qsem = _l2norm(qsem)
        ip_n = _l2norm(ip_ehs)
        sem = jnp.einsum('bhse,bne->bhsn', qsem, ip_n)
        sem = jax.lax.stop_gradient(sem)
        fused = attn_scores + SEM_SCALE * sem
        probs_ip = jax.nn.softmax(fused, axis=-1)
        probs_ip = probs_ip * spatial_mask[None, None, :, None]
        ip_out = jnp.einsum('bhsn,bhnd->bhsd', probs_ip, v_ip)
        ip_out = ip_out.transpose(0, 2, 1, 3).reshape(B, S, C)
        out = text_out + IP_SCALE * ip_out
        out = out @ W_out + b_out
        out = out + residual
        return out / RESCALE
    x = _L0_xattn_ref(x, ctx_2048, fside_S_0, L0_xattn_W_q, L0_xattn_W_k, L0_xattn_W_v, L0_xattn_W_k_ip, L0_xattn_W_v_ip, L0_xattn_W_out, L0_xattn_b_out)
    return x

_drawn_inputs = setup_inputs


def setup_inputs(seed=0):
    import zlib

    import numpy as np

    out = dict(_drawn_inputs(seed))
    spreads = {'L0_xattn_b_out': (0.0, 0.1)}
    factors = {}
    for name, (base, spread) in spreads.items():
        noise = np.random.default_rng([zlib.crc32(name.encode()), seed]).standard_normal(out[name].shape)
        drawn = base * np.exp(spread * noise) if base else spread * noise
        out[name] = jnp.asarray(drawn.astype(out[name].dtype))
    for name, factor in factors.items():
        out[name] = (out[name] * factor).astype(out[name].dtype)
    return out
```

```python
from contextlib import ExitStack

import concourse.bass as bass
from concourse import mybir

F32 = mybir.dt.float32
F32R = mybir.dt.float32r
F16 = mybir.dt.float16
I32 = mybir.dt.int32
ALU = mybir.AluOpType
ACT = mybir.ActivationFunctionType
AX = mybir.AxisListType
RMAX = bass.bass_isa.ReduceOp.max

HEADS = 20
N_IP = 4
SEM_SCALE = 0.5
EPS = 1e-12
HG = 4
SUB = 4
TILE = 512
LN_PSCALE = 10.39720770839918
K_SCALE = 4.0
G_SCALE = 256.0
RSQRT_MAGIC = 1597463007.0
TINY = 1e-37


def xattn_kernel(nc, x, ctx_in, mask, W_q, W_k, W_v, W_kip, W_vip, W_out, b_out, out):
    B, S, C = x.shape
    T_ALL, E = ctx_in.shape[1:]
    T = T_ALL - N_IP
    DH = C // HEADS
    P = 128
    CC = C // P
    EC = E // P
    NI = S // TILE
    SLOTS = NI * CC
    UNITS = SLOTS * SUB
    GK = HG * T_ALL
    GT = HG * T
    XW = T + N_IP + 1 + DH
    COL_G, COL_ONE, COL_V = T, T + N_IP, T + N_IP + 1
    IPR = HEADS * N_IP
    HALF = C // 2
    SCALE = float(DH) ** -0.5

    kt_d = nc.dram_tensor("kt_d", (B, 2, P, CC, T_ALL), F32, kind="Internal").ap()
    x_d = nc.dram_tensor("x_d", (B, T, 2 * HEADS * XW), F16, kind="Internal").ap()
    vw_d = nc.dram_tensor("vw_d", (B, IPR + 1, 2, C), F32, kind="Internal").ap()
    inv_d = nc.dram_tensor("inv_d", (P, 2), F32, kind="Internal").ap()

    top = ExitStack()
    with top:
        def tensors(stack):
            def sb(name, shape, dt):
                return stack.enter_context(nc.sbuf_tensor(name, shape, dt))
            return sb

        sb = tensors(top)

        def psum(name, dt=F32, cols=512):
            return top.enter_context(nc.psum_tensor(name, [P, cols], dt))

        def sem(name):
            return top.enter_context(nc.semaphore(name))

        ps_S = [psum("ps_S0"), psum("ps_S1")]
        ps_U = [psum("ps_U0"), psum("ps_U1")]
        ps_Q = psum("ps_Q")
        ps_M = psum("ps_M")
        ps_PT = [psum("ps_PT0", F16, 1024), psum("ps_PT1", F16, 1024)]

        ident = sb("ident", [P, P], F32)
        ident16 = sb("ident16", [P, P], F16)
        wq = [sb("wq_hi", [P, CC, C], F32R), sb("wq_lo", [P, CC, C], F32R)]
        wo = [sb("wo_hi", [P, CC, C], F32R), sb("wo_lo", [P, CC, C], F32R)]
        mask_sb = sb("mask_sb", [P, S // P], F32)
        inv = sb("inv", [P, 2], F32)
        inv_sv, inv_eps = inv[:, 0:1], inv[:, 1:2]

        prologue(nc, top, locals())
        main_loop(nc, top, locals())


def prologue(nc, top, g):
    P, B, S, C, E, T, T_ALL, CC, EC = (g[k] for k in "P B S C E T T_ALL CC EC".split())
    XW, COL_G, COL_ONE, COL_V, IPR, HALF, DH = (g[k] for k in "XW COL_G COL_ONE COL_V IPR HALF DH".split())
    ps_S, ps_U, ps_Q, ps_M = g["ps_S"], g["ps_U"], g["ps_Q"], g["ps_M"]
    ident, ident16, wq, wo, mask_sb, inv_sv, inv_eps = (
        g[k] for k in "ident ident16 wq wo mask_sb inv_sv inv_eps".split())
    kt_d, x_d, vw_d, ctx_in = g["kt_d"], g["x_d"], g["vw_d"], g["ctx_in"]

    stack = ExitStack()
    with stack:
        def sb(name, shape, dt):
            return stack.enter_context(nc.sbuf_tensor(name, shape, dt))

        def sem(name):
            return stack.enter_context(nc.semaphore(name))

        w_k = sb("w_k", [P, EC, C], F32)
        w_v = sb("w_v", [P, EC, C], F32)
        w_ip = sb("w_ip", [P, EC, C], F32)
        w_raw = sb("w_raw", [P, CC, C], F32)
        ctx_sb = sb("ctx_sb", [T_ALL, B, E], F32)
        ctxT = sb("ctxT", [P, EC, B, T_ALL], F32)
        ip16 = sb("ip16", [B * N_IP, E], F32)
        ipn = sb("ipn", [B * N_IP, E], F32)
        ipnT = sb("ipnT", [P, EC, B * N_IP], F32)
        ss = sb("ss", [P, 16], F32)
        kt = [sb("kt_hi", [P, CC, B, T_ALL], F32R), sb("kt_lo", [P, CC, B, T_ALL], F32R)]
        v_raw = sb("v_raw", [T, B, C], F32)
        kg_raw = sb("kg_raw", [T, B, T_ALL], F32)
        amax = sb("amax", [P, 8], F32)
        xb = sb("xb", [T, 2, HEADS, XW], F16)
        kg16 = sb("kg16", [T, 2, T_ALL + 1], F16)
        vip_bd = sb("vip_bd", [P, CC, B, IPR], F32)
        vw = [w_k[0:IPR, part * B:(part + 1) * B, :].bitcast(F32R) for part in range(2)]
        b_raw = sb("b_raw", [1, C], F32)
        b_sp = [sb("b_hi", [1, C], F32R), sb("b_lo", [1, C], F32R)]

        ld_ctx, ld_ip, ld_wk, ld_wkip, ld_wv, ld_wvip, ld_wq, ld_wo, ld_b, ld_mask = (
            sem(n) for n in "ld_ctx ld_ip ld_wk ld_wkip ld_wv ld_wvip ld_wq ld_wo ld_b ld_mask".split())
        zeroed, made_ident, tr_ready, tr_read, ipn_ready, ipt_ready, ipt_read = (
            sem(n) for n in "zeroed made_ident tr_ready tr_read ipn_ready ipt_ready ipt_read".split())
        k_ready, k_hi, k_lo, v_ready, v_read, kg_ready, kg_read = (
            sem(n) for n in "k_ready k_hi k_lo v_ready v_read kg_ready kg_read".split())
        vip_ready, vip_read, vw_ready, vw_hi, vw_lo = (
            sem(n) for n in "vip_ready vip_read vw_ready vw_hi vw_lo".split())
        wq_hi, wq_lo, wo_hi, wo_lo, b_hi, b_lo = (sem(n) for n in "pwq_hi pwq_lo pwo_hi pwo_lo pb_hi pb_lo".split())
        dve, local_max, all_max, x_built, stored, sq_ready, xstored = (
            sem(n) for n in "dve local_max all_max x_built stored sq_ready xstored".split())

        with nc.Block() as block:
            @block.sync
            def _(sp):
                sp.dma_start(ctx_sb[:], ctx_in.rearrange("b t e -> t b e")).then_inc(ld_ctx, 16)
                sp.dma_start(w_k[:], g["W_k"].rearrange("(c p) n -> p c n", p=P)).then_inc(ld_wk, 16)
                sp.dma_start(w_v[:], g["W_v"].rearrange("(c p) n -> p c n", p=P)).then_inc(ld_wv, 16)
                sp.dma_start(mask_sb[:], g["mask"].rearrange("(k p) -> p k", p=P), allow_slow_non_contiguous=True).then_inc(ld_mask, 16)
                sp.dma_start(b_raw[:], g["b_out"].rearrange("(a n) -> a n", a=1)).then_inc(ld_b, 16)
                sp.wait_ge(k_ready, CC)
                sp.dma_start(w_ip[:], g["W_vip"].rearrange("(c p) n -> p c n", p=P)).then_inc(ld_wvip, 16)
                sp.wait_ge(k_hi, 2 * CC)
                sp.wait_ge(k_lo, CC)
                for part in range(2):
                    for b in range(B):
                        sp.dma_start(kt_d[b, part], kt[part][:, :, b, :].bitcast(F32)).then_inc(stored, 16)
                for b in range(B):
                    sp.wait_ge(x_built, b + 1)
                    sp.dma_start(x_d[b], xb[:].rearrange("t k h w -> t (k h w)")).then_inc(xstored, 16)
                sp.wait_ge(b_hi, 1)
                sp.wait_ge(b_lo, 1)
                sp.wait_ge(vw_hi, 2 * B)
                sp.wait_ge(vw_lo, 2 * B)
                for part in range(2):
                    for b in range(B):
                        sp.dma_start(vw_d[b, 0:IPR, part], vw[part][:, b, :].bitcast(F32)).then_inc(stored, 16)
                        sp.dma_start(vw_d[b, IPR:IPR + 1, part], b_sp[part][:].bitcast(F32)).then_inc(stored, 16)
                sp.wait_ge(stored, 16 * (2 * B + 4 * B))
                sp.wait_ge(xstored, 16 * B)
                sp.wait_ge(ld_mask, 16)

            @block.gpsimd
            def _(pool):
                nc.gpsimd.memset(ident[:], 0.0).then_inc(zeroed, 1)
                nc.gpsimd.memset(ident16[:], 0.0).then_inc(zeroed, 1)
                pool.wait_ge(zeroed, 2)
                for one in (ident, ident16):
                    nc.gpsimd.affine_select(out=one[:], in_=one[:], compare_op=ALU.not_equal, fill=1.0, base=0,
                                            pattern=[[-1, P]], channel_multiplier=1).then_inc(made_ident, 1)
                for k in range(2):
                    pool.wait_ge(local_max, k + 1)
                    nc.gpsimd.partition_all_reduce(amax[:, 2 + k:3 + k], amax[:, k:k + 1], P, RMAX).then_inc(all_max, 1)

            @block.scalar
            def _(act):
                for b in range(B):
                    act.dma_start(ip16[b * N_IP:(b + 1) * N_IP, :], ctx_in[b, T:T_ALL, :]).then_inc(ld_ip, 16)
                act.dma_start(w_ip[:], g["W_kip"].rearrange("(c p) n -> p c n", p=P)).then_inc(ld_wkip, 16)
                act.dma_start(w_raw[:], g["W_q"].rearrange("(c p) n -> p c n", p=P)).then_inc(ld_wq, 16)
                act.wait_ge(ld_ip, 16 * B)
                nc.scalar.activation(ipn[:], ip16[:], ACT.Square, accum_out=ss[0:B * N_IP, 0:1]).then_inc(sq_ready, 1)
                for c in range(0, EC, 2):
                    act.wait_ge(tr_ready, c + 1)
                    nc.scalar.activation(ctxT[:, c].rearrange("p b t -> p (b t)"),
                                         ps_S[0][:, 0:B * T_ALL], ACT.Copy).then_inc(tr_read, 1)
                act.wait_ge(ld_wq, 16)
                nc.scalar.activation(wq[0][:], w_raw[:], ACT.Copy).then_inc(wq_hi, 1)
                for c in range(CC):
                    act.wait_ge(k_ready, c + 1)
                    psk = ps_U[c % 2]
                    nc.scalar.activation(kt[0][:, c, :, 0:T], psk[:, 0:B * T].rearrange("p (b t) -> p b t", b=B),
                                         ACT.Copy).then_inc(k_hi, 1)
                    nc.scalar.activation(kt[0][:, c, :, T:T_ALL],
                                         psk[:, B * T:B * T_ALL].rearrange("p (b n) -> p b n", b=B),
                                         ACT.Copy).then_inc(k_hi, 1)
                act.wait_ge(wq_hi, 1)
                act.wait_ge(wq_lo, 1)
                act.dma_start(w_raw[:], g["W_out"].rearrange("(c p) n -> p c n", p=P)).then_inc(ld_wo, 16)
                act.wait_ge(ld_wo, 16)
                nc.scalar.activation(wo[0][:], w_raw[:], ACT.Copy).then_inc(wo_hi, 1)
                act.wait_ge(ld_b, 16)
                nc.scalar.activation(b_sp[0][:], b_raw[:], ACT.Copy).then_inc(b_hi, 1)
                for n in range(2 * B):
                    b, h = divmod(n, 2)
                    act.wait_ge(vw_ready, n + 1)
                    nc.scalar.activation(vw[0][:, b, h * HALF:(h + 1) * HALF], ps_S[n % 2][0:IPR, 0:HALF],
                                         ACT.Copy).then_inc(vw_hi, 1)

            @block.vector
            def _(v):
                chain = [0]

                def link(ins):
                    chain[0] += 1
                    ins.then_inc(dve, 1)
                    v.wait_ge(dve, chain[0])

                link(nc.vector.memset(amax[:], 0.0))
                link(nc.vector.memset(vip_bd[:], 0.0))
                link(nc.vector.memset(kg16[:], 0.0))
                link(nc.vector.memset(kg16[:, 0, T_ALL:T_ALL + 1], 1.0))
                v.wait_ge(sq_ready, 1)
                n16 = B * N_IP
                sq, y, t = ss[0:n16, 1:2], ss[0:n16, 2:3], ss[0:n16, 3:4]
                link(nc.vector.tensor_scalar(sq, ss[0:n16, 0:1], TINY, None, ALU.max))
                link(nc.vector.tensor_scalar(y.bitcast(I32), sq.bitcast(I32), -0.5, RSQRT_MAGIC, ALU.mult, ALU.add))
                for _ in range(4):
                    link(nc.vector.tensor_tensor(t, y, y, ALU.mult))
                    link(nc.vector.scalar_tensor_tensor(out=t, in0=t, scalar=-0.5, in1=sq, op0=ALU.mult, op1=ALU.mult))
                    link(nc.vector.scalar_tensor_tensor(out=y, in0=t, scalar=1.5, in1=y, op0=ALU.add, op1=ALU.mult))
                link(nc.vector.tensor_scalar(y, y, 1.0 / EPS, None, ALU.min))
                nc.vector.tensor_scalar(ipn[:], ip16[:], y, None, ALU.mult).then_inc(ipn_ready, 1)
                for c in range(1, EC, 2):
                    v.wait_ge(tr_ready, c + 1)
                    nc.vector.tensor_copy(ctxT[:, c].rearrange("p b t -> p (b t)"),
                                          ps_S[1][:, 0:B * T_ALL]).then_inc(ipt_read, 1)
                v.wait_ge(ipt_ready, 1)
                nc.vector.tensor_copy(ipnT[:], ps_M[:, 0:EC * n16].rearrange("p (c n) -> p c n", c=EC)).then_inc(ipt_read, 1)
                v.wait_ge(ld_ctx, 16)
                link(nc.vector.tensor_reduce(amax[0:T_ALL, 4:5], ctx_sb[:].rearrange("t b e -> t (b e)"), AX.X, ALU.max,
                                             apply_absolute_value=True))
                nc.vector.tensor_copy(amax[0:T_ALL, 0:1], amax[0:T_ALL, 4:5]).then_inc(local_max, 1)
                v.wait_ge(wq_hi, 1)
                nc.vector.tensor_tensor(wq[1][:], w_raw[:], wq[0][:].bitcast(F32), ALU.subtract).then_inc(wq_lo, 1)
                for c in range(CC):
                    v.wait_ge(k_hi, 2 * c + 2)
                    psk = ps_U[c % 2]
                    link(nc.vector.tensor_tensor(kt[1][:, c, :, 0:T], psk[:, 0:B * T].rearrange("p (b t) -> p b t", b=B),
                                                 kt[0][:, c, :, 0:T].bitcast(F32), ALU.subtract))
                    nc.vector.tensor_tensor(kt[1][:, c, :, T:T_ALL],
                                            psk[:, B * T:B * T_ALL].rearrange("p (b n) -> p b n", b=B),
                                            kt[0][:, c, :, T:T_ALL].bitcast(F32), ALU.subtract).then_inc(k_lo, 1)
                for b in range(B):
                    v.wait_ge(kg_ready, b + 1)
                    nc.vector.tensor_copy(kg_raw[:, b, :], ps_M[0:T, 0:T_ALL]).then_inc(kg_read, 1)
                for n in range(2 * B):
                    b, h = divmod(n, 2)
                    v.wait_ge(v_ready, n + 1)
                    nc.vector.tensor_copy(v_raw[:, b, h * HALF:(h + 1) * HALF], ps_S[n % 2][0:T, 0:HALF]).then_inc(v_read, 1)
                v.wait_ge(v_read, 2 * B)
                v.wait_ge(kg_read, B)
                link(nc.vector.tensor_reduce(amax[0:T, 5:6], v_raw[:].rearrange("t b e -> t (b e)"), AX.X, ALU.max,
                                             apply_absolute_value=True))
                nc.vector.tensor_copy(amax[0:T, 1:2], amax[0:T, 5:6]).then_inc(local_max, 1)
                v.wait_ge(all_max, 2)
                link(nc.vector.tensor_scalar(ss[:, 4:6], amax[:, 2:4], 1e-30, None, ALU.max))
                link(nc.vector.tensor_scalar(ss[:, 4:6].bitcast(I32), ss[:, 4:6].bitcast(I32), 0x7F800000, None,
                                             ALU.bitwise_and))
                link(nc.vector.reciprocal(ss[:, 6:8], ss[:, 4:6]))
                link(nc.vector.tensor_scalar(ss[:, 8:9], ss[:, 6:7], ss[:, 6:7], K_SCALE, ALU.mult, ALU.mult))
                link(nc.vector.tensor_scalar(ss[:, 9:10], ss[:, 6:7], G_SCALE, None, ALU.mult))
                link(nc.vector.tensor_scalar(ss[:, 10:11], ss[:, 7:8], float(2 ** 14), None, ALU.mult))
                link(nc.vector.tensor_scalar(inv_sv, ss[:, 5:6], float(2 ** -14), None, ALU.mult))
                link(nc.vector.tensor_scalar(inv_eps, ss[:, 4:5], 1.0 / (EPS * G_SCALE), None, ALU.mult))
                for b in range(B):
                    if b:
                        v.wait_ge(xstored, 16 * b)
                    for lo_c, hi_c, sc in ((0, T, ss[0:T, 8:9]), (T, T_ALL, ss[0:T, 9:10])):
                        link(nc.vector.tensor_scalar(kg16[:, 0, lo_c:hi_c], kg_raw[:, b, lo_c:hi_c], sc, None, ALU.mult))
                        link(nc.vector.scalar_tensor_tensor(out=kg16[:, 1, lo_c:hi_c], in0=kg_raw[:, b, lo_c:hi_c],
                                                            scalar=sc, in1=kg16[:, 0, lo_c:hi_c],
                                                            op0=ALU.mult, op1=ALU.subtract))
                    for part in range(2):
                        link(nc.vector.tensor_copy(xb[:, part, :, 0:COL_V],
                                                   kg16[:, part, :].unsqueeze(1).to_broadcast([T, HEADS, COL_V])))
                    vr = v_raw[:, b, :].rearrange("t (h d) -> t h d", d=DH)
                    link(nc.vector.tensor_scalar(xb[:, 0, :, COL_V:XW], vr, ss[0:T, 10:11], None, ALU.mult))
                    nc.vector.scalar_tensor_tensor(out=xb[:, 1, :, COL_V:XW], in0=vr, scalar=ss[0:T, 10:11],
                                                   in1=xb[:, 0, :, COL_V:XW],
                                                   op0=ALU.mult, op1=ALU.subtract).then_inc(x_built, 1)
                v.wait_ge(wo_hi, 1)
                nc.vector.tensor_tensor(wo[1][:], w_raw[:], wo[0][:].bitcast(F32), ALU.subtract).then_inc(wo_lo, 1)
                v.wait_ge(b_hi, 1)
                nc.vector.tensor_tensor(b_sp[1][:], b_raw[:], b_sp[0][:].bitcast(F32), ALU.subtract).then_inc(b_lo, 1)
                v.wait_ge(vip_ready, 1)
                for c in range(CC):
                    for j in range(HG):
                        h = c * HG + j
                        last = nc.vector.tensor_copy(
                            vip_bd[j * DH:(j + 1) * DH, c, :, h * N_IP:(h + 1) * N_IP],
                            ps_M[j * DH:(j + 1) * DH, c * 16:(c + 1) * 16].rearrange("p (b n) -> p b n", b=B))
                        last.then_inc(vip_read, 1)
                for n in range(2 * B):
                    b, h = divmod(n, 2)
                    v.wait_ge(vw_hi, n + 1)
                    cols = slice(h * HALF, (h + 1) * HALF)
                    nc.vector.tensor_tensor(vw[1][:, b, cols], ps_S[n % 2][0:IPR, 0:HALF], vw[0][:, b, cols].bitcast(F32),
                                            ALU.subtract).then_inc(vw_lo, 1)

            @block.tensor
            def _(pe):
                pe.wait_ge(made_ident, 2)
                pe.wait_ge(ld_ctx, 16)
                for c in range(EC):
                    if c >= 2:
                        pe.wait_ge(tr_read if c % 2 == 0 else ipt_read, c // 2)
                    for b in range(B):
                        last = nc.tensor.transpose(ps_S[c % 2][:, b * T_ALL:(b + 1) * T_ALL],
                                                   ctx_sb[:, b, c * P:(c + 1) * P], ident[0:T_ALL, 0:T_ALL])
                    last.then_inc(tr_ready, 1)
                pe.wait_ge(ipn_ready, 1)
                n16 = B * N_IP
                for c in range(EC):
                    last = nc.tensor.transpose(ps_M[:, c * n16:(c + 1) * n16], ipn[:, c * P:(c + 1) * P],
                                               ident[0:n16, 0:n16])
                last.then_inc(ipt_ready, 1)
                pe.wait_ge(tr_read, EC // 2)
                pe.wait_ge(ipt_read, EC // 2 + 1)
                pe.wait_ge(ld_wk, 16)
                pe.wait_ge(ld_wkip, 16)
                for m in range(CC):
                    if m >= 2:
                        pe.wait_ge(k_lo, m - 1)
                    for lo_c, hi_c, t0, t1, w in ((0, B * T, 0, T, w_k), (B * T, B * T_ALL, T, T_ALL, w_ip)):
                        for c in range(EC):
                            last = nc.tensor.matmul(
                                ps_U[m % 2][:, lo_c:hi_c].rearrange("p (b t) -> p b t", b=B),
                                w[:, c, m * P:(m + 1) * P], ctxT[:, c, :, t0:t1], start=c == 0, stop=c == EC - 1)
                    last.then_inc(k_ready, 1)
                for b in range(B):
                    if b:
                        pe.wait_ge(kg_read, b)
                    for c in range(EC):
                        nc.tensor.matmul(ps_M[0:T, 0:T], ctxT[:, c, b, 0:T], ctxT[:, c, b, 0:T],
                                         start=c == 0, stop=c == EC - 1)
                    for c in range(EC):
                        last = nc.tensor.matmul(ps_M[0:T, T:T_ALL], ctxT[:, c, b, 0:T],
                                                ipnT[:, c, b * N_IP:(b + 1) * N_IP], start=c == 0, stop=c == EC - 1)
                    last.then_inc(kg_ready, 1)
                pe.wait_ge(ld_wv, 16)
                for n in range(2 * B):
                    b, h = divmod(n, 2)
                    if n >= 2:
                        pe.wait_ge(v_read, n - 1)
                    for c in range(EC):
                        last = nc.tensor.matmul(ps_S[n % 2][0:T, 0:HALF], ctxT[:, c, b, 0:T],
                                                w_v[:, c, h * HALF:(h + 1) * HALF], start=c == 0, stop=c == EC - 1)
                    last.then_inc(v_ready, 1)
                pe.wait_ge(ld_wvip, 16)
                pe.wait_ge(kg_read, B)
                for m in range(CC):
                    for c in range(EC):
                        last = nc.tensor.matmul(
                            ps_M[:, m * 16:(m + 1) * 16].rearrange("p (b t) -> p b t", b=B),
                            w_ip[:, c, m * P:(m + 1) * P], ctxT[:, c, :, T:T_ALL], start=c == 0, stop=c == EC - 1)
                last.then_inc(vip_ready, 1)
                pe.wait_ge(vip_read, HEADS)
                pe.wait_ge(ld_wo, 16)
                pe.wait_ge(v_read, 2 * B)
                for n in range(2 * B):
                    b, h = divmod(n, 2)
                    if n >= 2:
                        pe.wait_ge(vw_lo, n - 1)
                    for c in range(CC):
                        last = nc.tensor.matmul(ps_S[n % 2][0:IPR, 0:HALF], vip_bd[:, c, b, :],
                                                w_raw[:, c, h * HALF:(h + 1) * HALF], start=c == 0, stop=c == CC - 1)
                    last.then_inc(vw_ready, 1)


def main_loop(nc, top, g):
    P, B, S, C, T, T_ALL, CC = (g[k] for k in "P B S C T T_ALL CC".split())
    XW, COL_G, COL_ONE, COL_V, IPR, HALF, DH = (g[k] for k in "XW COL_G COL_ONE COL_V IPR HALF DH".split())
    NI, SLOTS, UNITS, GK, GT, SCALE = (g[k] for k in "NI SLOTS UNITS GK GT SCALE".split())
    ps_S, ps_U, ps_Q, ps_M, ps_PT = (g[k] for k in "ps_S ps_U ps_Q ps_M ps_PT".split())
    ident, ident16, wq, wo, mask_sb, inv_sv, inv_eps = (
        g[k] for k in "ident ident16 wq wo mask_sb inv_sv inv_eps".split())
    kt_d, x_d, vw_d, x, out = (g[k] for k in "kt_d x_d vw_d x out".split())
    AT_RING, X_RING, P_RING, H_RING = 8, 3, 4, 3
    LT, LU = 2, 3
    PASSES = ((0, 0), (0, 1), (1, 0))

    def sb(name, shape, dt):
        return top.enter_context(nc.sbuf_tensor(name, shape, dt))

    sems = []

    def sem(name):
        s = top.enter_context(nc.semaphore(name))
        sems.append(s)
        return s

    kbd = [sb("kbd_hi", [P, CC, GK], F32R), sb("kbd_lo", [P, CC, GK], F32R)]
    xm = sb("xm", [T, 2, HEADS, XW], F16)
    vw = sb("vw_sb", [IPR + 1, 2, C], F32R)
    xt_in = [sb(f"x_in{i}", [P, SUB, C], F32) for i in range(X_RING)]
    xT = [sb("xT_hi", [P, CC, TILE], F32R), sb("xT_lo", [P, CC, TILE], F32R)]
    qT = [[sb(f"qT{r}_{k}", [P, TILE], F32R) for k in range(2)] for r in range(2)]
    mneg = [sb(f"smax{i}", [P, HG], F32) for i in range(2)]
    sm = [sb(f"sm{i}", [P, HG, T], F32) for i in range(2)]
    s_ip = [sb(f"s_ip{i}", [P, SUB * HG, N_IP], F32) for i in range(3)]
    pr = [sb(f"pr{i}", [P, HG, T], F32) for i in range(P_RING)]
    ph = [[sb(f"ph{i}_{k}", [P, HG, T], F16) for k in range(2)] for i in range(H_RING)]
    pts = [sb(f"pts{i}", [T, HG, 2, P], F16) for i in range(2)]
    prod = [sb(f"prod{i}", [P, HG, T], F32) for i in range(2)]
    n2 = [sb(f"n2_{i}", [P, SUB * HG], F32) for i in range(2)]
    nd = [sb(f"nd{i}", [P, SUB * HG, N_IP + 1], F32) for i in range(2)]
    rd = [sb(f"rd{i}", [P, SUB * HG], F32) for i in range(2)]
    attn = [sb(f"attn{i}", [P, SUB, HG, DH], F32) for i in range(2)]
    aT = [[sb(f"aT{r}_{k}", [P, TILE], F32R) for k in range(2)] for r in range(AT_RING)]
    pip = [sb(f"pip{i}", [P, SUB, IPR + 1], F32) for i in range(2)]
    pipT = [sb(f"pipT{k}", [IPR + 1, TILE], F32R) for k in range(2)]
    NH = SUB * HG
    n2c, y, yt, rde, w, fmx, se = (sb(n, [P, NH], F32) for n in "n2c y yt rde w fmx se".split())
    f = sb("f", [P, NH, N_IP], F32)
    ef = sb("ef", [P, NH, N_IP], F32)

    x_loaded = [sem(f"x_loaded{i}") for i in range(X_RING)]
    x_stored = [sem(f"x_stored{i}") for i in range(X_RING)]
    consts, zero_kbd = sem("consts"), sem("zero_kbd")
    xT_ready, xT_hi, xT_lo = sem("xT_ready"), sem("xT_hi_done"), sem("xT_lo_done")
    q_ready, q_hi, q_lo = sem("q_ready"), sem("q_hi_done"), sem("q_lo_done")
    s_ready, max_done, sm_ready, s_read = sem("s_ready"), sem("max_done"), sem("sm_ready"), sem("s_read")
    p_ready, ph_ready, pl_ready = sem("p_ready"), sem("ph_ready"), sem("pl_ready")
    pt_ready, pts_ready = sem("pt_ready"), sem("pts_ready")
    u_ready, prod_done, n2_done, nd_done, rd_done, attn_ready = (
        sem(n) for n in "u_ready prod_done n2_done nd_done rd_done attn_ready".split())
    aT_ready, aT_hi, aT_lo = sem("aT_ready"), sem("aT_hi_done"), sem("aT_lo_done")
    y0_ready, y_ready, pool_step, f_step, f_ready, ef_ready, rs_ready, pip_ready = (
        sem(n) for n in "y0_ready y_ready pool_step f_step f_ready ef_ready rs_ready pip_ready".split())
    pT_ready, pT_hi, pT_lo = sem("pT_ready"), sem("pT_hi_done"), sem("pT_lo_done")
    o_ready, o_added = sem("o_ready"), sem("o_added")

    OUT_AT = {(6, 3): [(0, "M")], (7, 1): [(1, "M")], (7, 2): [(2, "Q")], (7, 3): [(3, "M")],
              (9, 1): [(4, "M")], (9, 2): [(5, "Q"), (6, "M")], (9, 3): [(7, "M")]}
    XT_AT = {1: [(0, "M"), (1, "Q")], 2: [(2, "M"), (3, "Q")], 3: [(4, "M")]}
    END_SLOT = SLOTS + 5
    bank = {"M": ps_M, "Q": ps_Q}

    def extras(slot, s):
        todo = []
        i, k = divmod(slot, CC)
        if s == 0 and slot + 1 < SLOTS:
            todo.append(("q", slot + 1, 0, "Q"))
        if s == 0 and 0 <= slot - 2 < SLOTS:
            todo.append(("attn", slot - 2, 0, "M"))
        if k == 3 and i + 1 < NI:
            todo += [("x", i + 1, c, m) for c, m in XT_AT.get(s, [])]
        if k == 1 and s == 2 and 0 <= i - 1 < NI:
            todo.append(("ip", i - 1, 0, "M"))
        for back in range(3):
            j = i - back
            if 0 <= j < NI:
                todo += [("out", j, h, m) for h, m in OUT_AT.get((k + CC * back, s), [])]
        return todo

    def steps():
        for slot in range(END_SLOT):
            for s in range(SUB):
                yield SUB * slot + s, slot, s

    with nc.Fori(0, B) as b:
        with nc.Block() as block:
            xb_dram = x[bass.ds(b, 1)].rearrange("a (i s p) c -> a i p s c", s=SUB, p=P)
            ob_dram = out[bass.ds(b, 1)].rearrange("a (i s p) c -> a i s p c", s=SUB, p=P)

            @block.sync
            def _(sp):
                def load(i):
                    if i >= X_RING:
                        sp.wait_ge(x_stored[i % X_RING], 16 * SUB * (i // X_RING))
                    sp.dma_start(xt_in[i % X_RING][:], xb_dram[0, i]).then_inc(x_loaded[i % X_RING], 16)

                for i in range(min(X_RING, NI)):
                    load(i)
                for i in range(NI):
                    for s in range(SUB):
                        sp.wait_ge(o_added, 2 * SUB * i + 2 * s + 2)
                        sp.dma_start(ob_dram[0, i, s], xt_in[i % X_RING][:, s, :]).then_inc(x_stored[i % X_RING], 16)
                    if i + X_RING < NI:
                        load(i + X_RING)
                for r in range(X_RING):
                    n = len(range(r, NI, X_RING))
                    sp.wait_ge(x_stored[r], 16 * SUB * n)

            @block.scalar
            def _(act):
                act.wait_ge(zero_kbd, 2)
                for part in range(2):
                    for j in range(HG):
                        rows = slice(j * DH, (j + 1) * DH)
                        act.dma_start(kbd[part][rows, :, j * T_ALL:(j + 1) * T_ALL].bitcast(F32),
                                      kt_d[bass.ds(b, 1)].rearrange("a k p c t -> (a k) p c t")[part, rows]).then_inc(consts, 16)
                act.dma_start(xm[:].rearrange("t k h w -> t (k h w)"),
                              x_d[bass.ds(b, 1)].rearrange("a t w -> (a t) w")).then_inc(consts, 16)
                act.dma_start(vw[:].bitcast(F32), vw_d[bass.ds(b, 1)].rearrange("a r k c -> (a r) k c")).then_inc(consts, 16)

                def x_chunk(i, c, m):
                    act.wait_ge(xT_ready, CC * i + c + 1)
                    if i:
                        act.wait_ge(q_ready, CC * i)
                    nc.scalar.activation(xT[0][:, c, :], bank[m][:], ACT.Copy).then_inc(xT_hi, 1)

                def q_chunk(n):
                    act.wait_ge(q_ready, n + 1)
                    if n >= 2:
                        act.wait_ge(s_ready, SUB * (n - 1))
                    nc.scalar.activation(qT[n % 2][0][:], ps_Q[:], ACT.Copy).then_inc(q_hi, 1)

                for c in range(CC):
                    x_chunk(0, c, "MQ"[c % 2])
                q_chunk(0)
                for t, slot, s in steps():
                    if t < UNITS:
                        act.wait_ge(sm_ready, t + 1)
                        if t >= P_RING:
                            act.wait_ge(prod_done, t - P_RING + 1)
                            act.wait_ge(pl_ready, t - P_RING + 1)
                        nc.scalar.activation(pr[t % P_RING][:], sm[t % 2][:], ACT.Exp, bias=LN_PSCALE,
                                             scale=SCALE).then_inc(p_ready, 1)
                    u = t - LT
                    if 0 <= u < UNITS:
                        act.wait_ge(pt_ready, u + 1)
                        if u >= 2:
                            act.wait_ge(u_ready, u - 1)
                        nc.scalar.activation(pts[u % 2][:].rearrange("t h k p -> t (h k p)"), ps_PT[u % 2][0:T, :],
                                             ACT.Copy).then_inc(pts_ready, 1)
                    for kind, i, c, m in extras(slot, s):
                        if kind == "x":
                            x_chunk(i, c, m)
                        elif kind == "q":
                            q_chunk(i)
                        elif kind == "attn":
                            act.wait_ge(aT_ready, i + 1)
                            if i >= AT_RING:
                                act.wait_ge(o_ready, 2 * SUB * ((i - AT_RING) // CC + 1))
                            nc.scalar.activation(aT[i % AT_RING][0][:], ps_M[:], ACT.Copy, scale=inv_sv).then_inc(aT_hi, 1)
                        elif kind == "ip":
                            act.wait_ge(pT_ready, i + 1)
                            if i:
                                act.wait_ge(o_ready, 2 * SUB * i)
                            nc.scalar.activation(pipT[0][:], ps_M[0:IPR + 1, :], ACT.Copy).then_inc(pT_hi, 1)
                    n = slot - 2
                    if s == 0 and 0 <= n < SLOTS:
                        act.wait_ge(f_ready, n + 1)
                        if n:
                            act.wait_ge(pip_ready, n)
                        nc.scalar.activation(ef[:], f[:], ACT.Exp, scale=SCALE).then_inc(ef_ready, 1)
                act.wait_ge(consts, 16 * (2 * HG + 2))

            @block.gpsimd
            def _(pool):
                nc.gpsimd.memset(kbd[0][:].bitcast(F32), 0.0).then_inc(zero_kbd, 1)
                nc.gpsimd.memset(kbd[1][:].bitcast(F32), 0.0).then_inc(zero_kbd, 1)
                for one in pip:
                    nc.gpsimd.memset(one[:, :, IPR:IPR + 1], 1.0).then_inc(zero_kbd, 1)
                done = [0]

                def link(ins):
                    done[0] += 1
                    ins.then_inc(pool_step, 1)
                    pool.wait_ge(pool_step, done[0])

                for t, slot, s in steps():
                    if t < UNITS:
                        pool.wait_ge(ph_ready, t + 1)
                        if t >= H_RING:
                            pool.wait_ge(pt_ready, t - H_RING + 1)
                        nc.gpsimd.tensor_tensor(ph[t % H_RING][1][:], pr[t % P_RING][:], ph[t % H_RING][0][:],
                                                ALU.subtract).then_inc(pl_ready, 1)
                    n = slot - 1
                    if s == 3 and 0 <= n < SLOTS:
                        pool.wait_ge(y0_ready, n + 1)
                        for it in range(3):
                            link(nc.gpsimd.tensor_tensor(yt[:], y[:], y[:], ALU.mult))
                            link(nc.gpsimd.tensor_tensor(yt[:], yt[:], n2c[:], ALU.mult))
                            link(nc.gpsimd.tensor_scalar(yt[:], yt[:], -0.5, 1.5, ALU.mult, ALU.add))
                            last = nc.gpsimd.tensor_tensor(y[:], y[:], yt[:], ALU.mult)
                            if it < 2:
                                link(last)
                        last.then_inc(y_ready, 1)
                    n = slot - 2
                    if s == 1 and 0 <= n < SLOTS:
                        i, k = divmod(n, CC)
                        pool.wait_ge(rs_ready, n + 1)
                        link(nc.gpsimd.tensor_tensor(
                            se[:].rearrange("p (s h) -> p s h", s=SUB), se[:].rearrange("p (s h) -> p s h", s=SUB),
                            mask_sb[:, i * SUB:(i + 1) * SUB].unsqueeze(2).to_broadcast([P, SUB, HG]), ALU.mult))
                        if i >= 2 and k == 0:
                            pool.wait_ge(pT_ready, i - 1)
                        nc.gpsimd.tensor_tensor(
                            pip[i % 2][:, :, k * HG * N_IP:(k + 1) * HG * N_IP].rearrange("p s (h n) -> p s h n", n=N_IP),
                            ef[:].rearrange("p (s h) n -> p s h n", s=SUB),
                            se[:].rearrange("p (s h) -> p s h", s=SUB).unsqueeze(3).to_broadcast([P, SUB, HG, N_IP]),
                            ALU.mult).then_inc(pip_ready, 1)

            @block.vector
            def _(v):
                fs = [0]

                def link(ins):
                    fs[0] += 1
                    ins.then_inc(f_step, 1)
                    v.wait_ge(f_step, fs[0])

                def lo_part(dst, src, hi, hi_done, n, signal):
                    v.wait_ge(hi_done, n)
                    nc.vector.tensor_tensor(dst, src, hi.bitcast(F32), ALU.subtract).then_inc(signal, 1)

                for c in range(CC):
                    lo_part(xT[1][:, c, :], bank["MQ"[c % 2]][:], xT[0][:, c, :], xT_hi, c + 1, xT_lo)
                lo_part(qT[0][1][:], ps_Q[:], qT[0][0][:], q_hi, 1, q_lo)
                for t, slot, s in steps():
                    if t < UNITS:
                        sc = ps_S[t % 2][:, 0:GK].rearrange("p (h t) -> p h t", h=HG)
                        v.wait_ge(s_ready, t + 1)
                        if t >= 2:
                            v.wait_ge(s_read, t - 1)
                        nc.vector.tensor_reduce(mneg[t % 2][:], sc[:, :, 0:T], AX.X, ALU.max).then_inc(max_done, 1)
                        if slot >= 3 and s == 0:
                            v.wait_ge(f_ready, slot - 2)
                        nc.vector.tensor_copy(s_ip[slot % 3][:, s * HG:(s + 1) * HG, :], sc[:, :, T:T_ALL]).then_inc(s_read, 1)
                        v.wait_ge(max_done, t + 1)
                        if t >= 2:
                            v.wait_ge(p_ready, t - 1)
                        nc.vector.tensor_tensor(sm[t % 2][:], sc[:, :, 0:T],
                                                mneg[t % 2][:].unsqueeze(2).to_broadcast([P, HG, T]),
                                                ALU.subtract).then_inc(sm_ready, 1)
                    u = t - LU
                    if 0 <= u < UNITS:
                        un, us = divmod(u, SUB)
                        hs = slice(us * HG, (us + 1) * HG)
                        uo = ps_U[u % 2][:, 0:HG * XW].rearrange("p (h w) -> p h w", h=HG)
                        v.wait_ge(u_ready, u + 1)
                        if un >= 2 and us == 0:
                            v.wait_ge(f_ready, un - 1)
                        nc.vector.tensor_copy(nd[un % 2][:, hs, :], uo[:, :, COL_G:COL_V]).then_inc(nd_done, 1)
                        if u >= 2:
                            v.wait_ge(n2_done, u - 1)
                        nc.vector.tensor_tensor(prod[u % 2][:], uo[:, :, 0:T], pr[u % P_RING][:],
                                                ALU.mult).then_inc(prod_done, 1)
                        v.wait_ge(nd_done, u + 1)
                        nc.vector.reciprocal(rd[un % 2][:, hs], nd[un % 2][:, hs, N_IP]).then_inc(rd_done, 1)
                        v.wait_ge(prod_done, u + 1)
                        if un >= 2 and us == 0:
                            v.wait_ge(y0_ready, un - 1)
                        nc.vector.tensor_reduce(n2[un % 2][:, hs], prod[u % 2][:], AX.X, ALU.add).then_inc(n2_done, 1)
                        v.wait_ge(rd_done, u + 1)
                        if un >= 2 and us == 0:
                            v.wait_ge(aT_ready, un - 1)
                        nc.vector.tensor_tensor(attn[un % 2][:, us], uo[:, :, COL_V:XW],
                                                rd[un % 2][:, hs].unsqueeze(2).to_broadcast([P, HG, DH]),
                                                ALU.mult).then_inc(attn_ready, 1)
                    if t < UNITS:
                        v.wait_ge(p_ready, t + 1)
                        if t >= H_RING:
                            v.wait_ge(pt_ready, t - H_RING + 1)
                            v.wait_ge(pl_ready, t - H_RING + 1)
                        nc.vector.tensor_copy(ph[t % H_RING][0][:], pr[t % P_RING][:]).then_inc(ph_ready, 1)
                    for kind, i, c, m in extras(slot, s):
                        if kind == "x":
                            lo_part(xT[1][:, c, :], bank[m][:], xT[0][:, c, :], xT_hi, CC * i + c + 1, xT_lo)
                        elif kind == "q":
                            lo_part(qT[i % 2][1][:], ps_Q[:], qT[i % 2][0][:], q_hi, i + 1, q_lo)
                        elif kind == "attn":
                            v.wait_ge(aT_hi, i + 1)
                            nc.vector.scalar_tensor_tensor(out=aT[i % AT_RING][1][:], in0=ps_M[:], scalar=inv_sv,
                                                           in1=aT[i % AT_RING][0][:].bitcast(F32),
                                                           op0=ALU.mult, op1=ALU.subtract).then_inc(aT_lo, 1)
                        elif kind == "ip":
                            lo_part(pipT[1][:], ps_M[0:IPR + 1, :], pipT[0][:], pT_hi, i + 1, pT_lo)
                        elif kind == "out":
                            n = 2 * SUB * i + c
                            v.wait_ge(o_ready, n + 1)
                            half = xt_in[i % X_RING][:, c // 2, (c % 2) * HALF:(c % 2 + 1) * HALF]
                            nc.vector.tensor_tensor(half, bank[m][:, 0:HALF], half, ALU.add).then_inc(o_added, 1)
                    n = slot - 1
                    if s == 2 and 0 <= n < SLOTS:
                        v.wait_ge(n2_done, SUB * (n + 1))
                        if n:
                            v.wait_ge(f_ready, n)
                        link(nc.vector.tensor_scalar(n2c[:], n2[n % 2][:], TINY, None, ALU.max))
                        nc.vector.tensor_scalar(y[:].bitcast(I32), n2c[:].bitcast(I32), -0.5, RSQRT_MAGIC,
                                                ALU.mult, ALU.add).then_inc(y0_ready, 1)
                        v.wait_ge(rd_done, SUB * (n + 1))
                        link(nc.vector.tensor_scalar(rde[:], rd[n % 2][:], inv_eps, None, ALU.mult))
                    n = slot - 2
                    if s == 0 and 0 <= n < SLOTS:
                        v.wait_ge(y_ready, n + 1)
                        if n:
                            v.wait_ge(ef_ready, n)
                        link(nc.vector.scalar_tensor_tensor(out=w[:], in0=y[:], scalar=K_SCALE ** 0.5 / G_SCALE,
                                                            in1=rde[:], op0=ALU.mult, op1=ALU.min))
                        link(nc.vector.tensor_tensor(f[:], nd[n % 2][:, :, 0:N_IP],
                                                     w[:].unsqueeze(2).to_broadcast([P, NH, N_IP]), ALU.mult))
                        link(nc.vector.scalar_tensor_tensor(out=f[:], in0=f[:], scalar=SEM_SCALE / SCALE,
                                                            in1=s_ip[n % 3][:], op0=ALU.mult, op1=ALU.add))
                        link(nc.vector.tensor_reduce(fmx[:], f[:], AX.X, ALU.max))
                        nc.vector.tensor_tensor(f[:], f[:], fmx[:].unsqueeze(2).to_broadcast([P, NH, N_IP]),
                                                ALU.subtract).then_inc(f_ready, 1)
                    if s == 1 and 0 <= n < SLOTS:
                        v.wait_ge(ef_ready, n + 1)
                        if n:
                            v.wait_ge(pip_ready, n)
                        link(nc.vector.tensor_reduce(se[:], ef[:], AX.X, ALU.add))
                        nc.vector.reciprocal(se[:], se[:]).then_inc(rs_ready, 1)

            @block.tensor
            def _(pe):
                freed = {"M": None, "Q": None}

                def take(m, signal, value):
                    if freed[m] is not None:
                        pe.wait_ge(*freed[m])
                    freed[m] = (signal, value)

                def x_chunk(i, c, m):
                    take(m, xT_lo, CC * i + c + 1)
                    for s in range(SUB):
                        last = nc.tensor.transpose(bank[m][:, s * P:(s + 1) * P],
                                                   xt_in[i % X_RING][:, s, c * P:(c + 1) * P], ident[:])
                    last.then_inc(xT_ready, 1)

                def q_chunk(n):
                    i, k = divmod(n, CC)
                    take("Q", q_lo, n + 1)
                    pe.wait_ge(xT_hi, CC * (i + 1))
                    pe.wait_ge(xT_lo, CC * (i + 1))
                    for c in range(CC):
                        for a, m in PASSES:
                            last = nc.tensor.matmul(ps_Q[:], wq[a][:, c, k * P:(k + 1) * P], xT[m][:, c, :],
                                                    start=c == 0 and (a, m) == (0, 0),
                                                    stop=c == CC - 1 and (a, m) == (1, 0))
                    last.then_inc(q_ready, 1)

                pe.wait_ge(x_loaded[0], 16)
                for c in range(CC):
                    x_chunk(0, c, "MQ"[c % 2])
                q_chunk(0)
                pe.wait_ge(consts, 16 * (2 * HG + 2))
                pe.wait_ge(zero_kbd, 4)
                for t, slot, s in steps():
                    if t < UNITS:
                        if s == 0:
                            pe.wait_ge(q_lo, slot + 1)
                        if t >= 2:
                            pe.wait_ge(sm_ready, t - 1)
                        for a, m in PASSES:
                            last = nc.tensor.matmul(ps_S[t % 2][:, 0:GK], qT[slot % 2][a][:, s * P:(s + 1) * P],
                                                    kbd[m][:, slot % CC, :], start=(a, m) == (0, 0),
                                                    stop=(a, m) == (1, 0))
                        last.then_inc(s_ready, 1)
                    u = t - LT
                    if 0 <= u < UNITS:
                        pe.wait_ge(ph_ready, u + 1)
                        pe.wait_ge(pl_ready, u + 1)
                        if u >= 2:
                            pe.wait_ge(pts_ready, u - 1)
                        for h in range(HG):
                            for k in range(2):
                                last = nc.tensor.transpose(ps_PT[u % 2][0:T, (2 * h + k) * P:(2 * h + k + 1) * P],
                                                           ph[u % H_RING][k][:, h, :], ident16[:])
                        last.then_inc(pt_ready, 1)
                    u = t - LU
                    if 0 <= u < UNITS:
                        k0 = (u // SUB) % CC
                        pe.wait_ge(pts_ready, u + 1)
                        if u >= 2:
                            pe.wait_ge(attn_ready, u - 1)
                        for h in range(HG):
                            for a, m in PASSES:
                                last = nc.tensor.matmul(ps_U[u % 2][:, h * XW:(h + 1) * XW], pts[u % 2][:, h, a, :],
                                                        xm[:, m, k0 * HG + h, :], start=(a, m) == (0, 0),
                                                        stop=(a, m) == (1, 0))
                        last.then_inc(u_ready, 1)
                    for kind, i, c, m in extras(slot, s):
                        if kind == "x":
                            if c == 0:
                                pe.wait_ge(x_loaded[i % X_RING], 16 * (i // X_RING + 1))
                            x_chunk(i, c, m)
                        elif kind == "q":
                            q_chunk(i)
                        elif kind == "attn":
                            pe.wait_ge(attn_ready, SUB * (i + 1))
                            take(m, aT_lo, i + 1)
                            for q in range(SUB):
                                last = nc.tensor.transpose(ps_M[:, q * P:(q + 1) * P],
                                                           attn[i % 2][:, q].rearrange("p h d -> p (h d)"), ident[:])
                            last.then_inc(aT_ready, 1)
                        elif kind == "ip":
                            pe.wait_ge(pip_ready, CC * (i + 1))
                            take(m, pT_lo, i + 1)
                            for q in range(SUB):
                                last = nc.tensor.transpose(ps_M[0:IPR + 1, q * P:(q + 1) * P], pip[i % 2][:, q, :],
                                                           ident[:])
                            last.then_inc(pT_ready, 1)
                        elif kind == "out":
                            take(m, o_added, 2 * SUB * i + c + 1)
                            pe.wait_ge(aT_lo, CC * (i + 1))
                            pe.wait_ge(pT_lo, i + 1)
                            q, h = divmod(c, 2)
                            cols = slice(h * HALF, (h + 1) * HALF)
                            for k in range(CC):
                                for a, w_ in PASSES:
                                    nc.tensor.matmul(bank[m][:, 0:HALF],
                                                     aT[(CC * i + k) % AT_RING][a][:, q * P:(q + 1) * P],
                                                     wo[w_][:, k, cols], start=k == 0 and (a, w_) == (0, 0), stop=False)
                            for a, w_ in PASSES:
                                last = nc.tensor.matmul(bank[m][:, 0:HALF], pipT[a][:, q * P:(q + 1) * P],
                                                        vw[:, w_, cols], start=False, stop=(a, w_) == (1, 0))
                            last.then_inc(o_ready, 1)

        nums = sorted(s.num for s in sems)
        assert nums == list(range(nums[0], nums[-1] + 1))
        nc.all_engine_barrier(sems_to_clear=range(nums[0], nums[-1] + 1))


_INS = ["x", "ctx_2048", "fside_S_0", "L0_xattn_W_q", "L0_xattn_W_k", "L0_xattn_W_v", "L0_xattn_W_k_ip",
        "L0_xattn_W_v_ip", "L0_xattn_W_out", "L0_xattn_b_out"]


def kernel(**inputs):
    import numpy as _np
    import concourse.bacc as _bacc
    from concourse import mybir as _mybir
    from concourse.bass_utils import run_bass_kernel_spmd as _run

    nc = _bacc.Bacc("TRN2", target_bir_lowering=False, num_devices=1)
    arrays, args = {}, []
    for name in _INS:
        a = _np.ascontiguousarray(inputs[name])
        arrays[f"in_{name}_dram"] = a
        args.append(nc.dram_tensor(f"in_{name}_dram", a.shape, _mybir.dt.from_np(a.dtype), kind="ExternalInput").ap())
    args.append(nc.dram_tensor("out_0_dram", inputs["x"].shape, _mybir.dt.float32, kind="ExternalOutput").ap())
    xattn_kernel(nc, *args)
    r = _run(nc, [arrays], core_ids=[0])
    return r.results[0]["out_0_dram"]
```

```python
from contextlib import ExitStack

import concourse.bass as bass
from concourse import mybir

F32 = mybir.dt.float32
F32R = mybir.dt.float32r
F16 = mybir.dt.float16
I32 = mybir.dt.int32
ALU = mybir.AluOpType
ACT = mybir.ActivationFunctionType
AX = mybir.AxisListType
RMAX = bass.bass_isa.ReduceOp.max

HEADS = 20
N_IP = 4
SEM_SCALE = 0.5
EPS = 1e-12
HG = 4
SUB = 4
TILE = 512
LN_PSCALE = 10.39720770839918
K_SCALE = 4.0
G_SCALE = 256.0
RSQRT_MAGIC = 1597463007.0
TINY = 1e-37


def xattn_kernel(nc, x, ctx_in, mask, W_q, W_k, W_v, W_kip, W_vip, W_out, b_out, out):
    B, S, C = x.shape
    T_ALL, E = ctx_in.shape[1:]
    T = T_ALL - N_IP
    DH = C // HEADS
    P = 128
    CC = C // P
    EC = E // P
    NI = S // TILE
    SLOTS = NI * CC
    GK = HG * T_ALL
    XW = T + N_IP + 1 + DH
    COL_G, COL_ONE, COL_V = T, T + N_IP, T + N_IP + 1
    IPR = HEADS * N_IP
    HALF = C // 2
    SCALE = float(DH) ** -0.5

    kt_d = nc.dram_tensor("kt_d", (B, CC, 2, P, T_ALL), F32, kind="Internal").ap()
    x_d = nc.dram_tensor("x_d", (B, T, 2, HEADS, XW), F16, kind="Internal").ap()
    vw_d = nc.dram_tensor("vw_d", (B, IPR + 1, 2, C), F32, kind="Internal").ap()

    top = ExitStack()
    with top:
        def tensors(stack):
            def sb(name, shape, dt):
                return stack.enter_context(nc.sbuf_tensor(name, shape, dt))
            return sb

        sb = tensors(top)

        def psum(name, dt=F32, cols=512):
            return top.enter_context(nc.psum_tensor(name, [P, cols], dt))

        def sem(name):
            return top.enter_context(nc.semaphore(name))

        ps_S = [psum("ps_S0"), psum("ps_S1")]
        ps_U = [psum("ps_U0"), psum("ps_U1")]
        ps_Q = psum("ps_Q")
        ps_M = psum("ps_M")
        ps_O = psum("ps_O")
        ps_PT = psum("ps_PT", F16, 1024)

        ident = sb("ident", [P, P], F32)
        ident16 = sb("ident16", [P, P], F16)
        wq = [sb("wq_hi", [P, CC, C], F32R), sb("wq_lo", [P, CC, C], F32R)]
        wo = [sb("wo_hi", [P, CC, C], F32R), sb("wo_lo", [P, CC, C], F32R)]
        mask_sb = sb("mask_sb", [P, S // P], F32)
        inv = sb("inv", [P, 2], F32)
        inv_sv, inv_eps = inv[:, 0:1], inv[:, 1:2]

        prologue(nc, top, locals())
        main_loop(nc, top, locals())


def prologue(nc, top, g):
    P, B, S, C, E, T, T_ALL, CC, EC = (g[k] for k in "P B S C E T T_ALL CC EC".split())
    XW, COL_G, COL_ONE, COL_V, IPR, HALF, DH = (g[k] for k in "XW COL_G COL_ONE COL_V IPR HALF DH".split())
    ps_S, ps_U, ps_Q, ps_M = g["ps_S"], g["ps_U"], g["ps_Q"], g["ps_M"]
    ident, ident16, wq, wo, mask_sb, inv_sv, inv_eps = (
        g[k] for k in "ident ident16 wq wo mask_sb inv_sv inv_eps".split())
    kt_d, x_d, vw_d, ctx_in = g["kt_d"], g["x_d"], g["vw_d"], g["ctx_in"]

    stack = ExitStack()
    with stack:
        def sb(name, shape, dt):
            return stack.enter_context(nc.sbuf_tensor(name, shape, dt))

        def sem(name):
            return stack.enter_context(nc.semaphore(name))

        w_k = sb("w_k", [P, EC, C], F32)
        w_v = sb("w_v", [P, EC, C], F32)
        w_ip = sb("w_ip", [P, EC, C], F32)
        w_raw = sb("w_raw", [P, CC, C], F32)
        ctx_sb = sb("ctx_sb", [T_ALL, B, E], F32)
        ctxT = sb("ctxT", [P, EC, B, T_ALL], F32)
        ip16 = sb("ip16", [B * N_IP, E], F32)
        ipn = sb("ipn", [B * N_IP, E], F32)
        ipnT = sb("ipnT", [P, EC, B * N_IP], F32)
        ss = sb("ss", [P, 16], F32)
        kt = [sb("kt_hi", [P, CC, B, T_ALL], F32R), sb("kt_lo", [P, CC, B, T_ALL], F32R)]
        v_raw = sb("v_raw", [T, B, C], F32)
        kg_raw = sb("kg_raw", [T, B, T_ALL], F32)
        amax = sb("amax", [P, 8], F32)
        xb = sb("xb", [T, 2, HEADS, XW], F16)
        kg16 = sb("kg16", [T, 2, T_ALL + 1], F16)
        vip_bd = sb("vip_bd", [P, CC, B, IPR], F32)
        vw = [w_k[0:IPR, part * B:(part + 1) * B, :].bitcast(F32R) for part in range(2)]
        b_raw = sb("b_raw", [1, C], F32)
        b_sp = [sb("b_hi", [1, C], F32R), sb("b_lo", [1, C], F32R)]

        ld_ctx, ld_ip, ld_wk, ld_wkip, ld_wv, ld_wvip, ld_wq, ld_wo, ld_b, ld_mask = (
            sem(n) for n in "ld_ctx ld_ip ld_wk ld_wkip ld_wv ld_wvip ld_wq ld_wo ld_b ld_mask".split())
        zeroed, made_ident, tr_ready, tr_read, ipn_ready, ipt_ready, ipt_read = (
            sem(n) for n in "zeroed made_ident tr_ready tr_read ipn_ready ipt_ready ipt_read".split())
        k_ready, k_hi, k_lo, v_ready, v_read, kg_ready, kg_read = (
            sem(n) for n in "k_ready k_hi k_lo v_ready v_read kg_ready kg_read".split())
        vip_ready, vip_read, vw_ready, vw_hi, vw_lo = (
            sem(n) for n in "vip_ready vip_read vw_ready vw_hi vw_lo".split())
        wq_hi, wq_lo, wo_hi, wo_lo, b_hi, b_lo = (sem(n) for n in "pwq_hi pwq_lo pwo_hi pwo_lo pb_hi pb_lo".split())
        dve, local_max, all_max, x_built, stored, sq_ready, xstored = (
            sem(n) for n in "dve local_max all_max x_built stored sq_ready xstored".split())

        with nc.Block() as block:
            @block.sync
            def _(sp):
                sp.dma_start(ctx_sb[:], ctx_in.rearrange("b t e -> t b e")).then_inc(ld_ctx, 16)
                sp.dma_start(w_k[:], g["W_k"].rearrange("(c p) n -> p c n", p=P)).then_inc(ld_wk, 16)
                sp.dma_start(w_v[:], g["W_v"].rearrange("(c p) n -> p c n", p=P)).then_inc(ld_wv, 16)
                sp.dma_start(mask_sb[:], g["mask"].rearrange("(k p) -> p k", p=P), allow_slow_non_contiguous=True).then_inc(ld_mask, 16)
                sp.dma_start(b_raw[:], g["b_out"].rearrange("(a n) -> a n", a=1)).then_inc(ld_b, 16)
                sp.wait_ge(k_ready, CC)
                sp.dma_start(w_ip[:], g["W_vip"].rearrange("(c p) n -> p c n", p=P)).then_inc(ld_wvip, 16)
                sp.wait_ge(k_hi, 2 * CC)
                sp.wait_ge(k_lo, CC)
                for part in range(2):
                    for b in range(B):
                        sp.dma_start(kt_d[b, :, part].rearrange("c p t -> p c t"), kt[part][:, :, b, :].bitcast(F32)).then_inc(stored, 16)
                for b in range(B):
                    sp.wait_ge(x_built, b + 1)
                    sp.dma_start(x_d[b], xb[:]).then_inc(xstored, 16)
                sp.wait_ge(b_hi, 1)
                sp.wait_ge(b_lo, 1)
                sp.wait_ge(vw_hi, 2 * B)
                sp.wait_ge(vw_lo, 2 * B)
                for part in range(2):
                    for b in range(B):
                        sp.dma_start(vw_d[b, 0:IPR, part], vw[part][:, b, :].bitcast(F32)).then_inc(stored, 16)
                        sp.dma_start(vw_d[b, IPR:IPR + 1, part], b_sp[part][:].bitcast(F32)).then_inc(stored, 16)
                sp.wait_ge(stored, 16 * (2 * B + 4 * B))
                sp.wait_ge(xstored, 16 * B)
                sp.wait_ge(ld_mask, 16)

            @block.gpsimd
            def _(pool):
                nc.gpsimd.memset(ident[:], 0.0).then_inc(zeroed, 1)
                nc.gpsimd.memset(ident16[:], 0.0).then_inc(zeroed, 1)
                pool.wait_ge(zeroed, 2)
                for one in (ident, ident16):
                    nc.gpsimd.affine_select(out=one[:], in_=one[:], compare_op=ALU.not_equal, fill=1.0, base=0,
                                            pattern=[[-1, P]], channel_multiplier=1).then_inc(made_ident, 1)
                for k in range(2):
                    pool.wait_ge(local_max, k + 1)
                    nc.gpsimd.partition_all_reduce(amax[:, 2 + k:3 + k], amax[:, k:k + 1], P, RMAX).then_inc(all_max, 1)

            @block.scalar
            def _(act):
                for b in range(B):
                    act.dma_start(ip16[b * N_IP:(b + 1) * N_IP, :], ctx_in[b, T:T_ALL, :]).then_inc(ld_ip, 16)
                act.dma_start(w_ip[:], g["W_kip"].rearrange("(c p) n -> p c n", p=P)).then_inc(ld_wkip, 16)
                act.dma_start(w_raw[:], g["W_q"].rearrange("(c p) n -> p c n", p=P)).then_inc(ld_wq, 16)
                act.wait_ge(ld_ip, 16 * B)
                nc.scalar.activation(ipn[:], ip16[:], ACT.Square, accum_out=ss[0:B * N_IP, 0:1]).then_inc(sq_ready, 1)
                for c in range(0, EC, 2):
                    act.wait_ge(tr_ready, c + 1)
                    nc.scalar.activation(ctxT[:, c].rearrange("p b t -> p (b t)"),
                                         ps_S[0][:, 0:B * T_ALL], ACT.Copy).then_inc(tr_read, 1)
                act.wait_ge(ld_wq, 16)
                nc.scalar.activation(wq[0][:], w_raw[:], ACT.Copy).then_inc(wq_hi, 1)
                for c in range(CC):
                    act.wait_ge(k_ready, c + 1)
                    psk = ps_U[c % 2]
                    nc.scalar.activation(kt[0][:, c, :, 0:T], psk[:, 0:B * T].rearrange("p (b t) -> p b t", b=B),
                                         ACT.Copy).then_inc(k_hi, 1)
                    nc.scalar.activation(kt[0][:, c, :, T:T_ALL],
                                         psk[:, B * T:B * T_ALL].rearrange("p (b n) -> p b n", b=B),
                                         ACT.Copy).then_inc(k_hi, 1)
                act.wait_ge(wq_hi, 1)
                act.wait_ge(wq_lo, 1)
                act.dma_start(w_raw[:], g["W_out"].rearrange("(c p) n -> p c n", p=P)).then_inc(ld_wo, 16)
                act.wait_ge(ld_wo, 16)
                nc.scalar.activation(wo[0][:], w_raw[:], ACT.Copy).then_inc(wo_hi, 1)
                act.wait_ge(ld_b, 16)
                nc.scalar.activation(b_sp[0][:], b_raw[:], ACT.Copy).then_inc(b_hi, 1)
                for n in range(2 * B):
                    b, h = divmod(n, 2)
                    act.wait_ge(vw_ready, n + 1)
                    nc.scalar.activation(vw[0][:, b, h * HALF:(h + 1) * HALF], ps_S[n % 2][0:IPR, 0:HALF],
                                         ACT.Copy).then_inc(vw_hi, 1)

            @block.vector
            def _(v):
                chain = [0]

                def link(ins):
                    chain[0] += 1
                    ins.then_inc(dve, 1)
                    v.wait_ge(dve, chain[0])

                link(nc.vector.memset(amax[:], 0.0))
                link(nc.vector.memset(vip_bd[:], 0.0))
                link(nc.vector.memset(kg16[:], 0.0))
                link(nc.vector.memset(kg16[:, 0, T_ALL:T_ALL + 1], 1.0))
                v.wait_ge(sq_ready, 1)
                n16 = B * N_IP
                sq, y, t = ss[0:n16, 1:2], ss[0:n16, 2:3], ss[0:n16, 3:4]
                link(nc.vector.tensor_scalar(sq, ss[0:n16, 0:1], TINY, None, ALU.max))
                link(nc.vector.tensor_scalar(y.bitcast(I32), sq.bitcast(I32), -0.5, RSQRT_MAGIC, ALU.mult, ALU.add))
                for _ in range(4):
                    link(nc.vector.tensor_tensor(t, y, y, ALU.mult))
                    link(nc.vector.scalar_tensor_tensor(out=t, in0=t, scalar=-0.5, in1=sq, op0=ALU.mult, op1=ALU.mult))
                    link(nc.vector.scalar_tensor_tensor(out=y, in0=t, scalar=1.5, in1=y, op0=ALU.add, op1=ALU.mult))
                link(nc.vector.tensor_scalar(y, y, 1.0 / EPS, None, ALU.min))
                nc.vector.tensor_scalar(ipn[:], ip16[:], y, None, ALU.mult).then_inc(ipn_ready, 1)
                for c in range(1, EC, 2):
                    v.wait_ge(tr_ready, c + 1)
                    nc.vector.tensor_copy(ctxT[:, c].rearrange("p b t -> p (b t)"),
                                          ps_S[1][:, 0:B * T_ALL]).then_inc(ipt_read, 1)
                v.wait_ge(ipt_ready, 1)
                nc.vector.tensor_copy(ipnT[:], ps_M[:, 0:EC * n16].rearrange("p (c n) -> p c n", c=EC)).then_inc(ipt_read, 1)
                v.wait_ge(ld_ctx, 16)
                link(nc.vector.tensor_reduce(amax[0:T_ALL, 4:5], ctx_sb[:].rearrange("t b e -> t (b e)"), AX.X, ALU.max,
                                             apply_absolute_value=True))
                nc.vector.tensor_copy(amax[0:T_ALL, 0:1], amax[0:T_ALL, 4:5]).then_inc(local_max, 1)
                v.wait_ge(wq_hi, 1)
                nc.vector.tensor_tensor(wq[1][:], w_raw[:], wq[0][:].bitcast(F32), ALU.subtract).then_inc(wq_lo, 1)
                for c in range(CC):
                    v.wait_ge(k_hi, 2 * c + 2)
                    psk = ps_U[c % 2]
                    link(nc.vector.tensor_tensor(kt[1][:, c, :, 0:T], psk[:, 0:B * T].rearrange("p (b t) -> p b t", b=B),
                                                 kt[0][:, c, :, 0:T].bitcast(F32), ALU.subtract))
                    nc.vector.tensor_tensor(kt[1][:, c, :, T:T_ALL],
                                            psk[:, B * T:B * T_ALL].rearrange("p (b n) -> p b n", b=B),
                                            kt[0][:, c, :, T:T_ALL].bitcast(F32), ALU.subtract).then_inc(k_lo, 1)
                for b in range(B):
                    v.wait_ge(kg_ready, b + 1)
                    nc.vector.tensor_copy(kg_raw[:, b, :], ps_M[0:T, 0:T_ALL]).then_inc(kg_read, 1)
                for n in range(2 * B):
                    b, h = divmod(n, 2)
                    v.wait_ge(v_ready, n + 1)
                    nc.vector.tensor_copy(v_raw[:, b, h * HALF:(h + 1) * HALF], ps_S[n % 2][0:T, 0:HALF]).then_inc(v_read, 1)
                v.wait_ge(v_read, 2 * B)
                v.wait_ge(kg_read, B)
                link(nc.vector.tensor_reduce(amax[0:T, 5:6], v_raw[:].rearrange("t b e -> t (b e)"), AX.X, ALU.max,
                                             apply_absolute_value=True))
                nc.vector.tensor_copy(amax[0:T, 1:2], amax[0:T, 5:6]).then_inc(local_max, 1)
                v.wait_ge(all_max, 2)
                link(nc.vector.tensor_scalar(ss[:, 4:6], amax[:, 2:4], 1e-30, None, ALU.max))
                link(nc.vector.tensor_scalar(ss[:, 4:6].bitcast(I32), ss[:, 4:6].bitcast(I32), 0x7F800000, None,
                                             ALU.bitwise_and))
                link(nc.vector.reciprocal(ss[:, 6:8], ss[:, 4:6]))
                link(nc.vector.tensor_scalar(ss[:, 8:9], ss[:, 6:7], ss[:, 6:7], K_SCALE, ALU.mult, ALU.mult))
                link(nc.vector.tensor_scalar(ss[:, 9:10], ss[:, 6:7], G_SCALE, None, ALU.mult))
                link(nc.vector.tensor_scalar(ss[:, 10:11], ss[:, 7:8], float(2 ** 14), None, ALU.mult))
                link(nc.vector.tensor_scalar(inv_sv, ss[:, 5:6], float(2 ** -14), None, ALU.mult))
                link(nc.vector.tensor_scalar(inv_eps, ss[:, 4:5], 1.0 / (EPS * G_SCALE), None, ALU.mult))
                for b in range(B):
                    if b:
                        v.wait_ge(xstored, 16 * b)
                    for lo_c, hi_c, sc in ((0, T, ss[0:T, 8:9]), (T, T_ALL, ss[0:T, 9:10])):
                        link(nc.vector.tensor_scalar(kg16[:, 0, lo_c:hi_c], kg_raw[:, b, lo_c:hi_c], sc, None, ALU.mult))
                        link(nc.vector.scalar_tensor_tensor(out=kg16[:, 1, lo_c:hi_c], in0=kg_raw[:, b, lo_c:hi_c],
                                                            scalar=sc, in1=kg16[:, 0, lo_c:hi_c],
                                                            op0=ALU.mult, op1=ALU.subtract))
                    for part in range(2):
                        link(nc.vector.tensor_copy(xb[:, part, :, 0:COL_V],
                                                   kg16[:, part, :].unsqueeze(1).to_broadcast([T, HEADS, COL_V])))
                    vr = v_raw[:, b, :].rearrange("t (h d) -> t h d", d=DH)
                    link(nc.vector.tensor_scalar(xb[:, 0, :, COL_V:XW], vr, ss[0:T, 10:11], None, ALU.mult))
                    nc.vector.scalar_tensor_tensor(out=xb[:, 1, :, COL_V:XW], in0=vr, scalar=ss[0:T, 10:11],
                                                   in1=xb[:, 0, :, COL_V:XW],
                                                   op0=ALU.mult, op1=ALU.subtract).then_inc(x_built, 1)
                v.wait_ge(wo_hi, 1)
                nc.vector.tensor_tensor(wo[1][:], w_raw[:], wo[0][:].bitcast(F32), ALU.subtract).then_inc(wo_lo, 1)
                v.wait_ge(b_hi, 1)
                nc.vector.tensor_tensor(b_sp[1][:], b_raw[:], b_sp[0][:].bitcast(F32), ALU.subtract).then_inc(b_lo, 1)
                v.wait_ge(vip_ready, 1)
                for c in range(CC):
                    for j in range(HG):
                        h = c * HG + j
                        last = nc.vector.tensor_copy(
                            vip_bd[j * DH:(j + 1) * DH, c, :, h * N_IP:(h + 1) * N_IP],
                            ps_M[j * DH:(j + 1) * DH, c * 16:(c + 1) * 16].rearrange("p (b n) -> p b n", b=B))
                        last.then_inc(vip_read, 1)
                for n in range(2 * B):
                    b, h = divmod(n, 2)
                    v.wait_ge(vw_hi, n + 1)
                    cols = slice(h * HALF, (h + 1) * HALF)
                    nc.vector.tensor_tensor(vw[1][:, b, cols], ps_S[n % 2][0:IPR, 0:HALF], vw[0][:, b, cols].bitcast(F32),
                                            ALU.subtract).then_inc(vw_lo, 1)

            @block.tensor
            def _(pe):
                pe.wait_ge(made_ident, 2)
                pe.wait_ge(ld_ctx, 16)
                for c in range(EC):
                    if c >= 2:
                        pe.wait_ge(tr_read if c % 2 == 0 else ipt_read, c // 2)
                    for b in range(B):
                        last = nc.tensor.transpose(ps_S[c % 2][:, b * T_ALL:(b + 1) * T_ALL],
                                                   ctx_sb[:, b, c * P:(c + 1) * P], ident[0:T_ALL, 0:T_ALL])
                    last.then_inc(tr_ready, 1)
                pe.wait_ge(ipn_ready, 1)
                n16 = B * N_IP
                for c in range(EC):
                    last = nc.tensor.transpose(ps_M[:, c * n16:(c + 1) * n16], ipn[:, c * P:(c + 1) * P],
                                               ident[0:n16, 0:n16])
                last.then_inc(ipt_ready, 1)
                pe.wait_ge(tr_read, EC // 2)
                pe.wait_ge(ipt_read, EC // 2 + 1)
                pe.wait_ge(ld_wk, 16)
                pe.wait_ge(ld_wkip, 16)
                for m in range(CC):
                    if m >= 2:
                        pe.wait_ge(k_lo, m - 1)
                    for lo_c, hi_c, t0, t1, w in ((0, B * T, 0, T, w_k), (B * T, B * T_ALL, T, T_ALL, w_ip)):
                        for c in range(EC):
                            last = nc.tensor.matmul(
                                ps_U[m % 2][:, lo_c:hi_c].rearrange("p (b t) -> p b t", b=B),
                                w[:, c, m * P:(m + 1) * P], ctxT[:, c, :, t0:t1], start=c == 0, stop=c == EC - 1)
                    last.then_inc(k_ready, 1)
                for b in range(B):
                    if b:
                        pe.wait_ge(kg_read, b)
                    for c in range(EC):
                        nc.tensor.matmul(ps_M[0:T, 0:T], ctxT[:, c, b, 0:T], ctxT[:, c, b, 0:T],
                                         start=c == 0, stop=c == EC - 1)
                    for c in range(EC):
                        last = nc.tensor.matmul(ps_M[0:T, T:T_ALL], ctxT[:, c, b, 0:T],
                                                ipnT[:, c, b * N_IP:(b + 1) * N_IP], start=c == 0, stop=c == EC - 1)
                    last.then_inc(kg_ready, 1)
                pe.wait_ge(ld_wv, 16)
                for n in range(2 * B):
                    b, h = divmod(n, 2)
                    if n >= 2:
                        pe.wait_ge(v_read, n - 1)
                    for c in range(EC):
                        last = nc.tensor.matmul(ps_S[n % 2][0:T, 0:HALF], ctxT[:, c, b, 0:T],
                                                w_v[:, c, h * HALF:(h + 1) * HALF], start=c == 0, stop=c == EC - 1)
                    last.then_inc(v_ready, 1)
                pe.wait_ge(ld_wvip, 16)
                pe.wait_ge(kg_read, B)
                for m in range(CC):
                    for c in range(EC):
                        last = nc.tensor.matmul(
                            ps_M[:, m * 16:(m + 1) * 16].rearrange("p (b t) -> p b t", b=B),
                            w_ip[:, c, m * P:(m + 1) * P], ctxT[:, c, :, T:T_ALL], start=c == 0, stop=c == EC - 1)
                last.then_inc(vip_ready, 1)
                pe.wait_ge(vip_read, HEADS)
                pe.wait_ge(ld_wo, 16)
                pe.wait_ge(v_read, 2 * B)
                for n in range(2 * B):
                    b, h = divmod(n, 2)
                    if n >= 2:
                        pe.wait_ge(vw_lo, n - 1)
                    for c in range(CC):
                        last = nc.tensor.matmul(ps_S[n % 2][0:IPR, 0:HALF], vip_bd[:, c, b, :],
                                                w_raw[:, c, h * HALF:(h + 1) * HALF], start=c == 0, stop=c == CC - 1)
                    last.then_inc(vw_ready, 1)


class Window:

    def __init__(self, b, first=False, last=False):
        self.b, self.first, self.last = b, first, last

    def has(self, n):
        return not (self.first and n < 0) and not (self.last and n >= 0)

    def count(self, per_batch, n):
        return self.b * per_batch + n


def main_loop(nc, top, g):
    P, B, S, C, T, T_ALL, CC = (g[k] for k in "P B S C T T_ALL CC".split())
    XW, COL_G, COL_ONE, COL_V, IPR, HALF, DH = (g[k] for k in "XW COL_G COL_ONE COL_V IPR HALF DH".split())
    NI, SLOTS, GK, SCALE = (g[k] for k in "NI SLOTS GK SCALE".split())
    ps_S, ps_U, ps_Q, ps_M, ps_O, ps_PT = (g[k] for k in "ps_S ps_U ps_Q ps_M ps_O ps_PT".split())
    ident, ident16, wq, wo, mask_sb, inv_sv, inv_eps = (
        g[k] for k in "ident ident16 wq wo mask_sb inv_sv inv_eps".split())
    kt_d, x_d, vw_d, x, out = (g[k] for k in "kt_d x_d vw_d x out".split())
    UNITS = SLOTS * SUB
    OUTS = 2 * SUB
    AT_RING, P_RING, SIP_RING = 2 * CC, 4, 4
    X_RING = NI
    assert NI == 4 and SLOTS % 4 == 0 and SLOTS % AT_RING == 0
    LT, LU = 2, 3
    PASSES = ((0, 0), (0, 1), (1, 0))
    Q_MMS = [(c, a, m) for c in range(CC) for a, m in PASSES]
    O_MMS = [(k, a, m) for k in range(CC + 1) for a, m in PASSES]
    Q_PIECE, O_PIECE = len(Q_MMS) // 3, len(O_MMS) // 2

    def sb(name, shape, dt):
        return top.enter_context(nc.sbuf_tensor(name, shape, dt))

    def sem(name):
        return top.enter_context(nc.semaphore(name))

    kbd = sb("kbd", [P, 2, CC, GK], F32R)
    xm = sb("xm", [T, 2, HEADS, XW], F16)
    vw = sb("vw_sb", [IPR + 1, 2, C], F32R)
    x_in = [sb(f"x_in{i}", [P, SUB, C], F32) for i in range(X_RING)]
    xT = [sb("xT_hi", [P, CC, TILE], F32R), sb("xT_lo", [P, CC, TILE], F32R)]
    qT = [[sb(f"qT{r}_{k}", [P, TILE], F32R) for k in range(2)] for r in range(2)]
    smax = [sb(f"smax{i}", [P, HG], F32) for i in range(2)]
    bias = [sb(f"bias{i}", [P, HG], F32) for i in range(2)]
    s_ip = [sb(f"s_ip{i}", [P, SUB * HG, N_IP], F32) for i in range(SIP_RING)]
    pr = [sb(f"pr{i}", [P, HG, T], F32) for i in range(P_RING)]
    ph = [[sb(f"ph{i}_{k}", [P, HG, T], F16) for k in range(2)] for i in range(2)]
    pts = [sb(f"pts{i}", [T, HG, 2, P], F16) for i in range(2)]
    n2 = [sb(f"n2_{i}", [P, SUB * HG], F32) for i in range(2)]
    nd = [sb(f"nd{i}", [P, SUB * HG, N_IP + 1], F32) for i in range(2)]
    rd = [sb(f"rd{i}", [P, SUB * HG], F32) for i in range(2)]
    attn = [sb(f"attn{i}", [P, SUB, HG, DH], F32) for i in range(2)]
    aT = [[sb(f"aT{r}_{k}", [P, TILE], F32R) for k in range(2)] for r in range(AT_RING)]
    pip = sb("pip", [P, SUB, IPR + 1], F32)
    pipT = [sb(f"pipT{k}", [IPR + 1, TILE], F32R) for k in range(2)]
    NH = SUB * HG
    n2h, y, yt, rde, w_sem, fmx, se, three_halves = (
        sb(n, [P, NH], F32) for n in "n2h y yt rde w_sem fmx se three_halves".split())
    f = sb("f", [P, NH, N_IP], F32)
    ef = sb("ef", [P, NH, N_IP], F32)

    x_loaded = [sem(f"x_loaded{i}") for i in range(X_RING)]
    x_stored = [sem(f"x_stored{i}") for i in range(X_RING)]
    kbd_loaded = [sem(f"kbd_loaded{k}") for k in range(CC)]
    xm_loaded = [sem(f"xm_loaded{k}") for k in range(CC)]
    vw_loaded, cleared = sem("vw_loaded"), sem("cleared")
    xT_ready, xT_hi, xT_lo = sem("xT_ready"), sem("xT_hi_done"), sem("xT_lo_done")
    q_ready, q_hi, q_lo = sem("q_ready"), sem("q_hi_done"), sem("q_lo_done")
    s_ready, max_done, s_read, bias_ready = sem("s_ready"), sem("max_done"), sem("s_read"), sem("bias_ready")
    p_ready, ph_ready, pl_ready = sem("p_ready"), sem("ph_ready"), sem("pl_ready")
    pt_ready, pts_ready = sem("pt_ready"), sem("pts_ready")
    u_ready, nd_done, prod_done, rd_done, n2_done, attn_ready = (
        sem(n) for n in "u_ready nd_done prod_done rd_done n2_done attn_ready".split())
    aT_ready, aT_hi, aT_lo = sem("aT_ready"), sem("aT_hi_done"), sem("aT_lo_done")
    n2h_done, y0_ready, newton_step, y_ready = (sem(n) for n in "n2h_done y0_ready newton_step y_ready".split())
    rde_done, f_step, f_ready, ef_ready, se_done, rs_ready, mask_done, pip_ready = (
        sem(n) for n in "rde_done f_step f_ready ef_ready se_done rs_ready mask_done pip_ready".split())
    pT_ready, pT_hi, pT_lo = sem("pT_ready"), sem("pT_hi_done"), sem("pT_lo_done")
    o_ready, o_added = sem("o_ready"), sem("o_added")
    bank = {"M": ps_M, "Q": ps_Q, "O": ps_O}

    Q_AT = {(4, 0): (1, 0), (4, 1): (1, 1), (4, 2): (1, 2), (4, 3): (2, 0), (0, 0): (1, 1), (0, 1): (1, 2),
            (0, 2): (2, 0), (0, 3): (2, 1), (1, 0): (1, 2), (1, 2): (2, 0), (1, 3): (2, 1), (2, 0): (1, 2),
            (2, 2): (2, 0), (2, 3): (2, 1), (3, 0): (1, 2)}
    OUT_AT = {(6, 3): (0, 0), (7, 0): (0, 1), (7, 1): (1, 0), (7, 2): (1, 1), (7, 3): (2, 0), (8, 0): (2, 1),
              (9, 1): (3, 0), (9, 2): (3, 1), (9, 3): (4, 0), (10, 0): (4, 1), (10, 1): (5, 0), (10, 2): (5, 1),
              (10, 3): (6, 0), (11, 0): (6, 1), (11, 1): (7, 0), (11, 2): (7, 1)}
    STORE_AT = {(7, 3): 0, (9, 3): 1, (10, 3): 2, (11, 3): 3}
    XT_AT = {2: [(0, "M"), (1, "O"), (2, "Q")], 3: [(3, "M"), (4, "O")]}
    FIRST, LAST, TAIL = -4, SLOTS - 4, 7

    def extras(w, slot, s):
        todo = []
        i, k = divmod(slot, CC)
        if s == 1 and w.has(slot - 2):
            todo.append(("attn", slot - 2, 0, 0, "M"))
        if (k, s) in Q_AT:
            ahead, part = Q_AT[k, s]
            if w.has(slot + ahead):
                todo.append(("q", slot + ahead, 0, part, "Q"))
        for back in range(3):
            if w.has(i - back) and (k + CC * back, s) in OUT_AT:
                todo.append(("out", i - back, *OUT_AT[k + CC * back, s], "O"))
        if k == 3 and w.has(i + 1):
            todo += [("x", i + 1, c, 0, m) for c, m in XT_AT.get(s, [])]
        if k == 1 and s == 2 and w.has(i - 1):
            todo.append(("ip", i - 1, 0, 0, "M"))
        return todo

    def before(slot, s):
        return (slot, s - 1) if s else (slot - 1, SUB - 1)

    def finished(w, slot, s):
        last_part = {"q": 2, "out": 1}
        return [e for e in extras(w, *before(slot, s)) if e[3] == last_part.get(e[0], 0)]

    def emptied(w, kind, i, c):
        return {"x": (xT_lo, w.count(SLOTS, CC * i + c + 1)), "q": (q_lo, w.count(SLOTS, i + 1)),
                "attn": (aT_lo, w.count(SLOTS, i + 1)), "ip": (pT_lo, w.count(NI, i + 1)),
                "out": (o_added, w.count(NI * OUTS, OUTS * i + c + 1))}[kind]

    def user_before(w, slot, s, entry):
        at = extras(w, slot, s)
        at = at[:at.index(entry)]
        for _ in range(UNITS):
            for e in reversed(at):
                if e[4] == entry[4]:
                    return e
            slot, s = before(slot, s)
            at = extras(w, slot, s)
        return None

    def steps(w):
        for slot in range(FIRST, TAIL if w.last else LAST):
            for s in range(SUB):
                yield SUB * slot + s, slot, s

    with nc.Block() as block:
        @block.sync
        def _(sp):
            def turn(w):
                def rows(dram, i):
                    return dram[bass.ds(w.b + i // NI, 1)].rearrange("a (i s p) c -> (a i) p s c", s=SUB, p=P)[i % NI]

                for t, slot, s in steps(w):
                    i, k = divmod(slot, CC)
                    if s == 0 and k == 1 and w.has(i + 1):
                        if w.has(i + 1 - X_RING):
                            sp.wait_ge(x_stored[(i + 1) % X_RING], w.count(16 * SUB, 0))
                        sp.dma_start(x_in[(i + 1) % X_RING][:], rows(x, i + 1)).then_inc(x_loaded[(i + 1) % X_RING], 16)
                    if s == 0 and FIRST <= slot < FIRST + CC and not w.last:
                        kg = slot - FIRST
                        if w.first and kg == 0:
                            sp.wait_ge(cleared, 3)
                        if w.has(SUB * slot - 1):
                            sp.wait_ge(s_ready, w.count(UNITS, SUB * slot))
                        for j in range(HG):
                            r = slice(j * DH, (j + 1) * DH)
                            sp.dma_start(kbd[r, :, kg, j * T_ALL:(j + 1) * T_ALL].bitcast(F32),
                                         kt_d[bass.ds(w.b, 1)].rearrange("a c k p t -> (a c) p k t")[kg, r]
                                         ).then_inc(kbd_loaded[kg], 16)
                    if s == 0 and FIRST < slot <= FIRST + CC and not w.last:
                        kg = slot - FIRST - 1
                        if w.has(SUB * (slot - 1) - 1):
                            sp.wait_ge(u_ready, w.count(UNITS, SUB * (slot - 1)))
                        sp.dma_start(xm[:, :, kg * HG:(kg + 1) * HG, :],
                                     x_d[bass.ds(w.b, 1)].rearrange("a t k h w -> (a t) k h w")[:, :, kg * HG:(kg + 1) * HG, :]
                                     ).then_inc(xm_loaded[kg], 16)
                    if s == 3 and slot == 6 and not w.last:
                        if w.has(-1):
                            sp.wait_ge(o_ready, w.count(NI * OUTS, 0))
                        sp.dma_start(vw[:].bitcast(F32),
                                     vw_d[bass.ds(w.b, 1)].rearrange("a r k c -> (a r) k c")).then_inc(vw_loaded, 16)
                    for back in (1, 2):
                        if w.has(i - back) and (k + CC * back, s) in STORE_AT:
                            j, q = i - back, STORE_AT[k + CC * back, s]
                            sp.wait_ge(o_added, w.count(NI * OUTS, OUTS * j + 2 * q + 2))
                            sp.dma_start(rows(out, j)[:, q], x_in[j % X_RING][:, q, :]).then_inc(x_stored[j % X_RING], 16)

            turn(Window(0, first=True))
            with sp.Fori(1, B) as b:
                turn(Window(b))
            turn(Window(B, last=True))
            for r in range(X_RING):
                sp.wait_ge(x_stored[r], 16 * SUB * B)

        @block.scalar
        def _(act):
            def turn(w):
                for t, slot, s in steps(w):
                    u = t - 1
                    if w.has(u):
                        act.wait_ge(p_ready, w.count(UNITS, u + 1))
                        if w.has(u - 2):
                            act.wait_ge(pt_ready, w.count(UNITS, u - 1))
                            act.wait_ge(pl_ready, w.count(UNITS, u - 1))
                        nc.scalar.activation(ph[u % 2][0][:], pr[u % P_RING][:], ACT.Copy).then_inc(ph_ready, 1)
                    for kind, i, c, _, m in finished(w, slot, s):
                        if kind == "x":
                            act.wait_ge(xT_ready, w.count(SLOTS, CC * i + c + 1))
                            if w.has(i - 1):
                                act.wait_ge(q_ready, w.count(SLOTS, CC * i))
                            nc.scalar.activation(xT[0][:, c, :], bank[m][:], ACT.Copy).then_inc(xT_hi, 1)
                        elif kind == "q":
                            act.wait_ge(q_ready, w.count(SLOTS, i + 1))
                            if w.has(i - 2):
                                act.wait_ge(s_ready, w.count(UNITS, SUB * (i - 1)))
                            nc.scalar.activation(qT[i % 2][0][:], ps_Q[:], ACT.Copy).then_inc(q_hi, 1)
                        elif kind == "attn":
                            act.wait_ge(aT_ready, w.count(SLOTS, i + 1))
                            if w.has(i - AT_RING):
                                act.wait_ge(o_ready, w.count(NI * OUTS, OUTS * ((i - AT_RING) // CC + 1)))
                            nc.scalar.activation(aT[i % AT_RING][0][:], ps_M[:], ACT.Copy, scale=inv_sv).then_inc(aT_hi, 1)
                        elif kind == "ip":
                            act.wait_ge(pT_ready, w.count(NI, i + 1))
                            if w.has(i - 1):
                                act.wait_ge(o_ready, w.count(NI * OUTS, OUTS * i))
                            nc.scalar.activation(pipT[0][:], ps_M[0:IPR + 1, :], ACT.Copy).then_inc(pT_hi, 1)
                    n = slot - 2
                    if s == 1 and w.has(n):
                        act.wait_ge(f_ready, w.count(SLOTS, n + 1))
                        if w.has(n - 1):
                            act.wait_ge(pip_ready, w.count(SLOTS, n))
                        nc.scalar.activation(ef[:], f[:], ACT.Exp, scale=SCALE).then_inc(ef_ready, 1)
                    u = t - LT
                    if w.has(u):
                        act.wait_ge(pt_ready, w.count(UNITS, u + 1))
                        if w.has(u - 2):
                            act.wait_ge(u_ready, w.count(UNITS, u - 1))
                        nc.scalar.activation(pts[u % 2][:].rearrange("t h k p -> t (h k p)"), ps_PT[0:T, :],
                                             ACT.Copy).then_inc(pts_ready, 1)
                    if w.has(t):
                        sc = ps_S[t % 2][:, 0:GK].rearrange("p (h t) -> p h t", h=HG)
                        act.wait_ge(bias_ready, w.count(UNITS, t + 1))
                        if w.has(t - P_RING):
                            act.wait_ge(n2_done, w.count(UNITS, t - P_RING + 1))
                        for h in range(HG):
                            last = nc.scalar.activation(pr[t % P_RING][:, h, :], sc[:, h, 0:T], ACT.Exp,
                                                        bias=bias[t % 2][:, h:h + 1], scale=SCALE)
                        last.then_inc(p_ready, 1)

            turn(Window(0, first=True))
            with act.Fori(1, B) as b:
                turn(Window(b))
            turn(Window(B, last=True))

        @block.gpsimd
        def _(pool):
            nc.gpsimd.memset(kbd[:].bitcast(F32), 0.0).then_inc(cleared, 1)
            nc.gpsimd.memset(pip[:, :, IPR:IPR + 1], 1.0).then_inc(cleared, 1)
            nc.gpsimd.memset(three_halves[:], 1.5).then_inc(cleared, 1)
            pool.wait_ge(cleared, 3)
            NEWTON = 3
            LINKS = 4 * NEWTON - 1

            def turn(w):
                for t, slot, s in steps(w):
                    u = t - 1
                    if w.has(u):
                        pool.wait_ge(ph_ready, w.count(UNITS, u + 1))
                        if w.has(u - 2):
                            pool.wait_ge(pt_ready, w.count(UNITS, u - 1))
                        nc.gpsimd.tensor_tensor(ph[u % 2][1][:], pr[u % P_RING][:], ph[u % 2][0][:],
                                                ALU.subtract).then_inc(pl_ready, 1)
                    n = slot - 1
                    if s == 3 and w.has(n):
                        pool.wait_ge(y0_ready, w.count(SLOTS, n + 1))
                        link = LINKS * n
                        for it in range(NEWTON):
                            nc.gpsimd.tensor_tensor(yt[:], y[:], y[:], ALU.mult).then_inc(newton_step, 1)
                            pool.wait_ge(newton_step, w.count(LINKS * SLOTS, link + 1))
                            nc.gpsimd.tensor_tensor(yt[:], yt[:], n2h[:], ALU.mult).then_inc(newton_step, 1)
                            pool.wait_ge(newton_step, w.count(LINKS * SLOTS, link + 2))
                            nc.gpsimd.tensor_tensor(yt[:], three_halves[:], yt[:], ALU.subtract).then_inc(newton_step, 1)
                            pool.wait_ge(newton_step, w.count(LINKS * SLOTS, link + 3))
                            step = nc.gpsimd.tensor_tensor(y[:], y[:], yt[:], ALU.mult)
                            if it < NEWTON - 1:
                                step.then_inc(newton_step, 1)
                                pool.wait_ge(newton_step, w.count(LINKS * SLOTS, link + 4))
                            else:
                                step.then_inc(y_ready, 1)
                            link += 4
                    n = slot - 2
                    if s == 1 and w.has(n):
                        i, k = divmod(n, CC)
                        pool.wait_ge(rs_ready, w.count(SLOTS, n + 1))
                        j = i % NI
                        nc.gpsimd.tensor_tensor(
                            se[:].rearrange("p (s h) -> p s h", s=SUB), se[:].rearrange("p (s h) -> p s h", s=SUB),
                            mask_sb[:, j * SUB:(j + 1) * SUB].unsqueeze(2).to_broadcast([P, SUB, HG]),
                            ALU.mult).then_inc(mask_done, 1)
                        pool.wait_ge(mask_done, w.count(SLOTS, n + 1))
                        if k == 0 and w.has(i - 1):
                            pool.wait_ge(pT_ready, w.count(NI, i))
                        nc.gpsimd.tensor_tensor(
                            pip[:, :, k * HG * N_IP:(k + 1) * HG * N_IP].rearrange("p s (h n) -> p s h n", n=N_IP),
                            ef[:].rearrange("p (s h) n -> p s h n", s=SUB),
                            se[:].rearrange("p (s h) -> p s h", s=SUB).unsqueeze(3).to_broadcast([P, SUB, HG, N_IP]),
                            ALU.mult).then_inc(pip_ready, 1)

            turn(Window(0, first=True))
            with pool.Fori(1, B) as b:
                turn(Window(b))
            turn(Window(B, last=True))

        @block.vector
        def _(v):
            def lo_part(dst, src, hi, hi_done, n, signal):
                v.wait_ge(hi_done, n)
                nc.vector.tensor_tensor(dst, src, hi.bitcast(F32), ALU.subtract).then_inc(signal, 1)

            def turn(w):
                def f_link(n, k):
                    v.wait_ge(f_step, w.count(4 * SLOTS, 4 * n + k))

                for t, slot, s in steps(w):
                    for kind, i, c, _, m in finished(w, slot, s):
                        if kind == "out":
                            v.wait_ge(o_ready, w.count(NI * OUTS, OUTS * i + c + 1))
                            half = x_in[i % X_RING][:, c // 2, (c % 2) * HALF:(c % 2 + 1) * HALF]
                            nc.vector.tensor_tensor(half, ps_O[:, 0:HALF], half, ALU.add).then_inc(o_added, 1)
                    if w.has(t):
                        sc = ps_S[t % 2][:, 0:GK].rearrange("p (h t) -> p h t", h=HG)
                        v.wait_ge(s_ready, w.count(UNITS, t + 1))
                        if w.has(t - 2):
                            v.wait_ge(bias_ready, w.count(UNITS, t - 1))
                        nc.vector.tensor_reduce(smax[t % 2][:], sc[:, :, 0:T], AX.X, ALU.max).then_inc(max_done, 1)
                        if s == 0 and w.has(slot - SIP_RING):
                            v.wait_ge(f_ready, w.count(SLOTS, slot - SIP_RING + 1))
                        nc.vector.tensor_copy(s_ip[slot % SIP_RING][:, s * HG:(s + 1) * HG, :],
                                              sc[:, :, T:T_ALL]).then_inc(s_read, 1)
                        v.wait_ge(max_done, w.count(UNITS, t + 1))
                        if w.has(t - 2):
                            v.wait_ge(p_ready, w.count(UNITS, t - 1))
                        nc.vector.tensor_scalar(bias[t % 2][:], smax[t % 2][:], -SCALE, LN_PSCALE,
                                                ALU.mult, ALU.add).then_inc(bias_ready, 1)
                    for kind, i, c, _, m in finished(w, slot, s):
                        if kind == "x":
                            lo_part(xT[1][:, c, :], bank[m][:], xT[0][:, c, :], xT_hi, w.count(SLOTS, CC * i + c + 1), xT_lo)
                        elif kind == "q":
                            lo_part(qT[i % 2][1][:], ps_Q[:], qT[i % 2][0][:], q_hi, w.count(SLOTS, i + 1), q_lo)
                        elif kind == "attn":
                            v.wait_ge(aT_hi, w.count(SLOTS, i + 1))
                            nc.vector.scalar_tensor_tensor(out=aT[i % AT_RING][1][:], in0=ps_M[:], scalar=inv_sv,
                                                           in1=aT[i % AT_RING][0][:].bitcast(F32),
                                                           op0=ALU.mult, op1=ALU.subtract).then_inc(aT_lo, 1)
                        elif kind == "ip":
                            lo_part(pipT[1][:], ps_M[0:IPR + 1, :], pipT[0][:], pT_hi, w.count(NI, i + 1), pT_lo)
                    m = slot - 2
                    logits = w.has(m)
                    if s == 1 and logits:
                        v.wait_ge(ef_ready, w.count(SLOTS, m + 1))
                        if w.has(m - 1):
                            v.wait_ge(pip_ready, w.count(SLOTS, m))
                        nc.vector.tensor_reduce(se[:], ef[:], AX.X, ALU.add).then_inc(se_done, 1)
                    u = t - LU
                    un, us = divmod(u, SUB)
                    hs = slice(us * HG, (us + 1) * HG)
                    uo = ps_U[u % 2][:, 0:HG * XW].rearrange("p (h w) -> p h w", h=HG)
                    if w.has(u):
                        v.wait_ge(u_ready, w.count(UNITS, u + 1))
                        nc.vector.tensor_copy(nd[un % 2][:, hs, :], uo[:, :, COL_G:COL_V]).then_inc(nd_done, 1)
                    if s == 1 and logits:
                        v.wait_ge(se_done, w.count(SLOTS, m + 1))
                        nc.vector.reciprocal(se[:], se[:]).then_inc(rs_ready, 1)
                    if s == 0 and logits:
                        v.wait_ge(y_ready, w.count(SLOTS, m + 1))
                        if w.has(m - 1):
                            v.wait_ge(ef_ready, w.count(SLOTS, m))
                        v.wait_ge(rde_done, w.count(SLOTS, m + 1))
                        nc.vector.scalar_tensor_tensor(out=w_sem[:], in0=y[:], scalar=K_SCALE ** 0.5 / G_SCALE,
                                                       in1=rde[:], op0=ALU.mult, op1=ALU.min).then_inc(f_step, 1)
                    if w.has(u):
                        v.wait_ge(pl_ready, w.count(UNITS, u + 1))
                        nc.vector.tensor_tensor(pr[u % P_RING][:], uo[:, :, 0:T], pr[u % P_RING][:],
                                                ALU.mult).then_inc(prod_done, 1)
                        v.wait_ge(nd_done, w.count(UNITS, u + 1))
                        nc.vector.reciprocal(rd[un % 2][:, hs], nd[un % 2][:, hs, N_IP]).then_inc(rd_done, 1)
                    if s == 0 and logits:
                        f_link(m, 1)
                        nc.vector.tensor_tensor(f[:], nd[m % 2][:, :, 0:N_IP],
                                                w_sem[:].unsqueeze(2).to_broadcast([P, NH, N_IP]),
                                                ALU.mult).then_inc(f_step, 1)
                    if w.has(u):
                        v.wait_ge(prod_done, w.count(UNITS, u + 1))
                        nc.vector.tensor_reduce(n2[un % 2][:, hs], pr[u % P_RING][:], AX.X, ALU.add).then_inc(n2_done, 1)
                    if s == 0 and logits:
                        f_link(m, 2)
                        nc.vector.scalar_tensor_tensor(out=f[:], in0=f[:], scalar=SEM_SCALE / SCALE,
                                                       in1=s_ip[m % SIP_RING][:], op0=ALU.mult, op1=ALU.add).then_inc(f_step, 1)
                    if w.has(u):
                        v.wait_ge(rd_done, w.count(UNITS, u + 1))
                        if w.has(un - 2) and us == 0:
                            v.wait_ge(aT_ready, w.count(SLOTS, un - 1))
                        nc.vector.tensor_tensor(attn[un % 2][:, us], uo[:, :, COL_V:XW],
                                                rd[un % 2][:, hs].unsqueeze(2).to_broadcast([P, HG, DH]),
                                                ALU.mult).then_inc(attn_ready, 1)
                    if s == 0 and logits:
                        f_link(m, 3)
                        nc.vector.tensor_reduce(fmx[:], f[:], AX.X, ALU.max).then_inc(f_step, 1)
                        f_link(m, 4)
                        nc.vector.tensor_tensor(f[:], f[:], fmx[:].unsqueeze(2).to_broadcast([P, NH, N_IP]),
                                                ALU.subtract).then_inc(f_ready, 1)
                    n = slot - 1
                    if s == 2 and w.has(n):
                        v.wait_ge(n2_done, w.count(UNITS, SUB * (n + 1)))
                        if w.has(n - 1):
                            v.wait_ge(f_ready, w.count(SLOTS, n))
                        nc.vector.tensor_scalar(n2h[:], n2[n % 2][:], TINY, 0.5, ALU.max, ALU.mult).then_inc(n2h_done, 1)
                        v.wait_ge(rd_done, w.count(UNITS, SUB * (n + 1)))
                        nc.vector.tensor_scalar(rde[:], rd[n % 2][:], inv_eps, None, ALU.mult).then_inc(rde_done, 1)
                        v.wait_ge(n2h_done, w.count(SLOTS, n + 1))
                        nc.vector.tensor_scalar(y[:].bitcast(I32), n2h[:].bitcast(I32), -0.5, RSQRT_MAGIC - 2 ** 22,
                                                ALU.mult, ALU.add).then_inc(y0_ready, 1)

            turn(Window(0, first=True))
            with v.Fori(1, B) as b:
                turn(Window(b))
            turn(Window(B, last=True))

        @block.tensor
        def _(pe):
            def turn(w):
                for t, slot, s in steps(w):
                    if w.has(t):
                        if s == 0:
                            pe.wait_ge(q_lo, w.count(SLOTS, slot + 1))
                            if 0 <= slot < CC:
                                pe.wait_ge(kbd_loaded[slot], w.count(16 * HG, 16 * HG))
                        if w.has(t - 2):
                            pe.wait_ge(s_read, w.count(UNITS, t - 1))
                            pe.wait_ge(p_ready, w.count(UNITS, t - 1))
                        for a, m in PASSES:
                            last = nc.tensor.matmul(ps_S[t % 2][:, 0:GK], qT[slot % 2][a][:, s * P:(s + 1) * P],
                                                    kbd[:, m, slot % CC, :], start=(a, m) == PASSES[0],
                                                    stop=(a, m) == PASSES[-1])
                        last.then_inc(s_ready, 1)
                    u = t - LT
                    if w.has(u):
                        pe.wait_ge(ph_ready, w.count(UNITS, u + 1))
                        pe.wait_ge(pl_ready, w.count(UNITS, u + 1))
                        if w.has(u - 1):
                            pe.wait_ge(pts_ready, w.count(UNITS, u))
                        for h in range(HG):
                            for k in range(2):
                                last = nc.tensor.transpose(ps_PT[0:T, (2 * h + k) * P:(2 * h + k + 1) * P],
                                                           ph[u % 2][k][:, h, :], ident16[:])
                        last.then_inc(pt_ready, 1)
                    u = t - LU
                    if w.has(u):
                        un, us = divmod(u, SUB)
                        k0 = un % CC
                        if us == 0 and 0 <= un % SLOTS < CC:
                            pe.wait_ge(xm_loaded[k0], w.count(16, 16 * (un // SLOTS + 1)))
                        pe.wait_ge(pts_ready, w.count(UNITS, u + 1))
                        if w.has(u - 2):
                            pe.wait_ge(attn_ready, w.count(UNITS, u - 1))
                        for h in range(HG):
                            for a, m in PASSES:
                                last = nc.tensor.matmul(ps_U[u % 2][:, h * XW:(h + 1) * XW], pts[u % 2][:, h, a, :],
                                                        xm[:, m, k0 * HG + h, :], start=(a, m) == PASSES[0],
                                                        stop=(a, m) == PASSES[-1])
                        last.then_inc(u_ready, 1)
                    for entry in extras(w, slot, s):
                        kind, i, c, part, m = entry
                        if part == 0:
                            was = user_before(w, slot, s, entry)
                            if was is not None:
                                pe.wait_ge(*emptied(w, *was[:3]))
                        if kind == "x":
                            if c == 0:
                                pe.wait_ge(x_loaded[i % X_RING], w.count(16, 16 * (i // NI + 1)))
                            for q in range(SUB):
                                last = nc.tensor.transpose(bank[m][:, q * P:(q + 1) * P],
                                                           x_in[i % X_RING][:, q, c * P:(c + 1) * P], ident[:])
                            last.then_inc(xT_ready, 1)
                        elif kind == "q":
                            ii, k = divmod(i, CC)
                            mms = Q_MMS[part * Q_PIECE:(part + 1) * Q_PIECE]
                            if k == 0:
                                pe.wait_ge(xT_lo, w.count(SLOTS, CC * ii + mms[-1][0] + 1))
                            for cc, a, b_ in mms:
                                last = nc.tensor.matmul(ps_Q[:], wq[a][:, cc, k * P:(k + 1) * P], xT[b_][:, cc, :],
                                                        start=(cc, a, b_) == Q_MMS[0], stop=(cc, a, b_) == Q_MMS[-1])
                            if part == 2:
                                last.then_inc(q_ready, 1)
                        elif kind == "attn":
                            pe.wait_ge(attn_ready, w.count(UNITS, SUB * (i + 1)))
                            for q in range(SUB):
                                last = nc.tensor.transpose(ps_M[:, q * P:(q + 1) * P],
                                                           attn[i % 2][:, q].rearrange("p h d -> p (h d)"), ident[:])
                            last.then_inc(aT_ready, 1)
                        elif kind == "ip":
                            pe.wait_ge(pip_ready, w.count(SLOTS, CC * (i + 1)))
                            if w.first and i == 0:
                                pe.wait_ge(cleared, 3)
                            for q in range(SUB):
                                last = nc.tensor.transpose(ps_M[0:IPR + 1, q * P:(q + 1) * P], pip[:, q, :], ident[:])
                            last.then_inc(pT_ready, 1)
                        elif kind == "out":
                            q, h = divmod(c, 2)
                            cols = slice(h * HALF, (h + 1) * HALF)
                            if part == 0:
                                pe.wait_ge(aT_lo, w.count(SLOTS, CC * (i + 1)))
                            else:
                                pe.wait_ge(pT_lo, w.count(NI, i + 1))
                                if c == 0 and i % NI == 0:
                                    pe.wait_ge(vw_loaded, w.count(16, 16 * (i // NI + 1)))
                            for k, a, b_ in O_MMS[part * O_PIECE:(part + 1) * O_PIECE]:
                                if k < CC:
                                    stationary, moving = aT[(CC * i + k) % AT_RING][a], wo[b_][:, k, cols]
                                else:
                                    stationary, moving = pipT[a], vw[:, b_, cols]
                                last = nc.tensor.matmul(ps_O[:, 0:HALF], stationary[:, q * P:(q + 1) * P], moving,
                                                        start=(k, a, b_) == O_MMS[0], stop=(k, a, b_) == O_MMS[-1])
                            if part == 1:
                                last.then_inc(o_ready, 1)

            turn(Window(0, first=True))
            with pe.Fori(1, B) as b:
                turn(Window(b))
            turn(Window(B, last=True))


_INS = ["x", "ctx_2048", "fside_S_0", "L0_xattn_W_q", "L0_xattn_W_k", "L0_xattn_W_v", "L0_xattn_W_k_ip",
        "L0_xattn_W_v_ip", "L0_xattn_W_out", "L0_xattn_b_out"]


def kernel(**inputs):
    import numpy as _np
    import concourse.bacc as _bacc
    from concourse import mybir as _mybir
    from concourse.bass_utils import run_bass_kernel_spmd as _run

    nc = _bacc.Bacc("TRN2", target_bir_lowering=False, num_devices=1)
    arrays, args = {}, []
    for name in _INS:
        a = _np.ascontiguousarray(inputs[name])
        arrays[f"in_{name}_dram"] = a
        args.append(nc.dram_tensor(f"in_{name}_dram", a.shape, _mybir.dt.from_np(a.dtype), kind="ExternalInput").ap())
    args.append(nc.dram_tensor("out_0_dram", inputs["x"].shape, _mybir.dt.float32, kind="ExternalOutput").ap())
    xattn_kernel(nc, *args)
    r = _run(nc, [arrays], core_ids=[0])
    return r.results[0]["out_0_dram"]
```

```python
from contextlib import ExitStack

import concourse.bass as bass
from concourse import mybir

F32 = mybir.dt.float32
F32R = mybir.dt.float32r
F16 = mybir.dt.float16
I32 = mybir.dt.int32
ALU = mybir.AluOpType
ACT = mybir.ActivationFunctionType
AX = mybir.AxisListType
RMAX = bass.bass_isa.ReduceOp.max

HEADS = 20
N_IP = 4
SEM_SCALE = 0.5
EPS = 1e-12
HG = 4
SUB = 4
TILE = 512
LN_PSCALE = 10.39720770839918
K_SCALE = 4.0
G_SCALE = 256.0
RSQRT_MAGIC = 1597463007.0
TINY = 1e-37


def xattn_kernel(nc, x, ctx_in, mask, W_q, W_k, W_v, W_kip, W_vip, W_out, b_out, out):
    B, S, C = x.shape
    T_ALL, E = ctx_in.shape[1:]
    T = T_ALL - N_IP
    DH = C // HEADS
    P = 128
    CC = C // P
    EC = E // P
    NI = S // TILE
    SLOTS = NI * CC
    GK = HG * T_ALL
    XW = T + N_IP + 1 + DH
    COL_G, COL_ONE, COL_V = T, T + N_IP, T + N_IP + 1
    SPLIT = P - T
    IPR = HEADS * N_IP
    HALF = C // 2
    SCALE = float(DH) ** -0.5

    kt_d = nc.dram_tensor("kt_d", (B, CC, 2, P, T_ALL), F32, kind="Internal").ap()
    x_d = nc.dram_tensor("x_d", (B, 2, P, HEADS, XW), F16, kind="Internal").ap()
    vw_d = nc.dram_tensor("vw_d", (B, IPR + 1, 2, C), F32, kind="Internal").ap()

    top = ExitStack()
    with top:
        def tensors(stack):
            def sb(name, shape, dt):
                return stack.enter_context(nc.sbuf_tensor(name, shape, dt))
            return sb

        sb = tensors(top)

        def psum(name, dt=F32, cols=512):
            return top.enter_context(nc.psum_tensor(name, [P, cols], dt))

        def sem(name):
            return top.enter_context(nc.semaphore(name))

        ps_S = [psum("ps_S0"), psum("ps_S1")]
        ps_U = [psum("ps_U0"), psum("ps_U1")]
        ps_Q = psum("ps_Q")
        ps_M = psum("ps_M")
        ps_O = psum("ps_O")
        ps_PT = psum("ps_PT", F16, 1024)

        ident = sb("ident", [P, P], F32)
        ident16 = sb("ident16", [P, P], F16)
        wq = [sb("wq_hi", [P, CC, C], F32R), sb("wq_lo", [P, CC, C], F32R)]
        wo = [sb("wo_hi", [P, CC, C], F32R), sb("wo_lo", [P, CC, C], F32R)]
        mask_sb = sb("mask_sb", [P, S // P], F32)
        inv = sb("inv", [P, 2], F32)
        inv_sv, inv_eps = inv[:, 0:1], inv[:, 1:2]

        x_in0 = sb("x_in0", [P, SUB, C], F32)
        x_loaded0 = sem("x_loaded0")

        prologue(nc, top, locals())
        main_loop(nc, top, locals())


def prologue(nc, top, g):
    P, B, S, C, E, T, T_ALL, CC, EC = (g[k] for k in "P B S C E T T_ALL CC EC".split())
    XW, COL_G, COL_ONE, COL_V, IPR, HALF, DH, SPLIT = (
        g[k] for k in "XW COL_G COL_ONE COL_V IPR HALF DH SPLIT".split())
    ps_S, ps_U, ps_Q, ps_M, ps_O = (g[k] for k in "ps_S ps_U ps_Q ps_M ps_O".split())
    ident, ident16, wq, wo, mask_sb, inv_sv, inv_eps = (
        g[k] for k in "ident ident16 wq wo mask_sb inv_sv inv_eps".split())
    kt_d, x_d, vw_d, ctx_in, x_in0, x_loaded0 = (g[k] for k in "kt_d x_d vw_d ctx_in x_in0 x_loaded0".split())
    GI = HG * N_IP
    N16 = B * N_IP

    stack = ExitStack()
    with stack:
        def sb(name, shape, dt):
            return stack.enter_context(nc.sbuf_tensor(name, shape, dt))

        def sem(name):
            return stack.enter_context(nc.semaphore(name))

        w_k = sb("w_k", [P, EC, C], F32)
        w_v = sb("w_v", [P, EC, C], F32)
        w_ip = sb("w_ip", [P, EC, C], F32)
        w_raw = sb("w_raw", [P, CC, C], F32)
        ctx_sb = sb("ctx_sb", [T_ALL, B, E], F32)
        ctxT = sb("ctxT", [P, EC, B, T_ALL], F32)
        ipn = sb("ipn", [N16, E], F32)
        ipT = sb("ipT", [P, EC, B, N_IP], F32)
        vip_sb = sb("vip_sb", [N16, C], F32)
        ss = sb("ss", [P, 16], F32)
        amax = sb("amax", [P, 16], F32)
        kt_hi = x_in0[:].rearrange("p s c -> p (s c)")[:, 0:CC * B * T_ALL]
        kt_hi = kt_hi.rearrange("p (c b t) -> p c b t", c=CC, b=B).bitcast(F32R)
        kt = [kt_hi, sb("kt_lo", [P, CC, B, T_ALL], F32R)]
        vT = sb("vT", [P, CC, B * T], F32)
        kg_raw = sb("kg_raw", [T, B, T_ALL], F32)
        kg16 = sb("kg16", [T, B, 2, T_ALL + 1], F16)
        vip_bd = sb("vip_bd", [P, CC, B, HG, N_IP], F32)
        xb = [sb("xb", [T, B // 2, 2, HEADS, XW], F16)]
        w_k16 = w_k[0:T].rearrange("p c n -> p (c n)").bitcast(F16)[:, 0:B * HEADS * XW]
        xb.append(w_k16.rearrange("t (b k h w) -> t b k h w", b=B // 2, k=2, w=XW))
        vw = [ctx_sb[0:B * GI].rearrange("t b e -> t (b e)")[:, 0:CC * C].rearrange("t (c n) -> t c n", c=CC).bitcast(F32R),
              w_v[0:B * GI, 0:CC, :].bitcast(F32R)]
        b_raw = w_v[0:1, CC, :]
        b_sp = [w_v[0:1, CC + 1 + k, :].bitcast(F32R) for k in range(2)]
        squares = vT[0:N16].rearrange("p c n -> p (c n)")[:, 0:E]

        ld_ctx, ld_ip, ld_wk, ld_wkip, ld_wv, ld_wvip, ld_wq, ld_wo, ld_b, ld_mask = (
            sem(n) for n in "ld_ctx ld_ip ld_wk ld_wkip ld_wv ld_wvip ld_wq ld_wo ld_b ld_mask".split())
        zeroed, made_ident, bd_zero, ip_ready, tr_ready, tr_even, tr_odd, ipn_ready, ipt_ready, ipt_read = (
            sem(n) for n in "zeroed made_ident bd_zero ip_ready tr_ready tr_even tr_odd ipn_ready ipt_ready ipt_read".split())
        k_ready, k_hi, k_lo, kg_ready, kg_read, kg16_hi, kg16_ready = (
            sem(n) for n in "k_ready k_hi k_lo kg_ready kg_read kg16_hi kg16_ready".split())
        vt_ready, vt_read, vt_max, v_ready, xg_hi, xv_hi, x_lo = (
            sem(n) for n in "vt_ready vt_read vt_max v_ready xg_hi xv_hi x_lo".split())
        vip_ready, vip_copied, vipt_ready, vip_read, vw_ready, vw_hi, vw_lo = (
            sem(n) for n in "vip_ready vip_copied vipt_ready vip_read vw_ready vw_hi vw_lo".split())
        wq_hi, wq_lo, wo_hi, wo_lo, b_hi, b_lo = (sem(n) for n in "pwq_hi pwq_lo pwo_hi pwo_lo pb_hi pb_lo".split())
        dve, local_max, all_max, scaled, kt_stored, stored, sq_ready = (
            sem(n) for n in "dve local_max all_max scaled kt_stored stored sq_ready".split())
        ps_vw = [ps_U[0], ps_U[1]]
        ps_vt = [ps_U[0], ps_U[1]]
        ps_v = [ps_S[0], ps_S[1], ps_O, ps_M]
        VC = (CC - 1) * P

        with nc.Block() as block:
            @block.sync
            def _(sp):
                sp.dma_start(ctx_sb[:], ctx_in.rearrange("b t e -> t b e")).then_inc(ld_ctx, 16)
                sp.dma_start(w_k[:], g["W_k"].rearrange("(c p) n -> p c n", p=P)).then_inc(ld_wk, 16)
                sp.dma_start(w_ip[:], g["W_kip"].rearrange("(c p) n -> p c n", p=P)).then_inc(ld_wkip, 16)
                sp.dma_start(w_raw[:], g["W_q"].rearrange("(c p) n -> p c n", p=P)).then_inc(ld_wq, 16)
                sp.dma_start(w_v[:], g["W_v"].rearrange("(c p) n -> p c n", p=P)).then_inc(ld_wv, 16)
                sp.dma_start(mask_sb[:], g["mask"].rearrange("(k p) -> p k", p=P),
                             allow_slow_non_contiguous=True).then_inc(ld_mask, 16)
                sp.wait_ge(k_ready, CC)
                sp.dma_start(w_ip[:], g["W_vip"].rearrange("(c p) n -> p c n", p=P)).then_inc(ld_wvip, 16)
                sp.wait_ge(wq_hi, 1)
                sp.wait_ge(wq_lo, 1)
                sp.dma_start(w_raw[:], g["W_out"].rearrange("(c p) n -> p c n", p=P)).then_inc(ld_wo, 16)
                sp.wait_ge(k_hi, 2 * CC)
                sp.wait_ge(k_lo, 2 * CC)
                for part in range(2):
                    for b in range(B):
                        sp.dma_start(kt_d[b, :, part].rearrange("c p t -> p c t"),
                                     kt[part][:, :, b, :].bitcast(F32)).then_inc(kt_stored, 16)
                sp.wait_ge(kt_stored, 16 * 2 * B)
                sp.dma_start(x_in0[:], g["x"][0, 0:TILE].rearrange("(s p) c -> p s c", p=P)).then_inc(x_loaded0, 16)
                sp.wait_ge(vt_ready, CC)
                sp.dma_start(b_raw, g["b_out"].rearrange("(a n) -> a n", a=1)).then_inc(ld_b, 16)
                for pair in range(B // 2):
                    for tile, row, part, lo_t, hi_t in ((0, 0, 0, 0, T), (0, T, 0, 0, SPLIT),
                                                        (1, 0, 0, SPLIT, T), (1, T - SPLIT, 1, 0, T)):
                        if part == 0:
                            sp.wait_ge(xv_hi, B + 2 * pair + 2)
                        else:
                            sp.wait_ge(x_lo, B + 2 * pair + 2)
                        sp.dma_start(x_d[2 * pair:2 * pair + 2, tile, row:row + hi_t - lo_t].rearrange("b t h w -> t b h w"),
                                     xb[pair][lo_t:hi_t, :, part]).then_inc(stored, 16)
                sp.wait_ge(b_hi, 1)
                sp.wait_ge(b_lo, 1)
                for part in range(2):
                    for b in range(B):
                        sp.dma_start(vw_d[b, IPR:IPR + 1, part], b_sp[part].bitcast(F32)).then_inc(stored, 16)
                for part, done in ((0, vw_hi), (1, vw_lo)):
                    sp.wait_ge(done, 2 * CC)
                    for b in range(B):
                        sp.dma_start(vw_d[b, 0:IPR, part].rearrange("(c r) n -> r c n", r=GI),
                                     vw[part][b * GI:(b + 1) * GI].bitcast(F32)).then_inc(stored, 16)
                sp.wait_ge(stored, 16 * (2 * B + 2 * B + 2 * B))
                sp.wait_ge(ld_mask, 16)

            @block.gpsimd
            def _(pool):
                nc.gpsimd.memset(ident[:], 0.0).then_inc(zeroed, 1)
                nc.gpsimd.memset(ident16[:], 0.0).then_inc(zeroed, 1)
                pool.wait_ge(zeroed, 2)
                for one in (ident, ident16):
                    nc.gpsimd.affine_select(out=one[:], in_=one[:], compare_op=ALU.not_equal, fill=1.0, base=0,
                                            pattern=[[-1, P]], channel_multiplier=1).then_inc(made_ident, 1)
                nc.gpsimd.memset(vip_bd[:], 0.0).then_inc(bd_zero, 1)
                for k in range(2):
                    pool.wait_ge(local_max, k + 1)
                    nc.gpsimd.partition_all_reduce(amax[:, 2 + k:3 + k], amax[:, k:k + 1], P, RMAX).then_inc(all_max, 1)

            @block.scalar
            def _(act):
                for b in range(B):
                    act.dma_start(ipn[b * N_IP:(b + 1) * N_IP, :], ctx_in[b, T:T_ALL, :]).then_inc(ld_ip, 16)
                for c in range(0, EC, 2):
                    act.wait_ge(tr_ready, c + 1)
                    nc.scalar.activation(ctxT[:, c].rearrange("p b t -> p (b t)"),
                                         ps_S[0][:, 0:B * T_ALL], ACT.Copy).then_inc(tr_even, 1)
                act.wait_ge(ld_ip, 16 * B)
                nc.scalar.activation(squares, ipn[:], ACT.Square, accum_out=ss[0:N16, 0:1]).then_inc(sq_ready, 1)
                for c in range(CC):
                    act.wait_ge(k_ready, c + 1)
                    psk = ps_U[c % 2]
                    nc.scalar.activation(kt[0][:, c, :, 0:T], psk[:, 0:B * T].rearrange("p (b t) -> p b t", b=B),
                                         ACT.Copy).then_inc(k_hi, 1)
                    nc.scalar.activation(kt[0][:, c, :, T:T_ALL],
                                         psk[:, B * T:B * T_ALL].rearrange("p (b n) -> p b n", b=B),
                                         ACT.Copy).then_inc(k_hi, 1)
                    if c == 1:
                        act.wait_ge(ld_wq, 16)
                        nc.scalar.activation(wq[0][:], w_raw[:], ACT.Copy).then_inc(wq_hi, 1)
                act.wait_ge(ld_wo, 16)
                nc.scalar.activation(wo[0][:], w_raw[:], ACT.Copy).then_inc(wo_hi, 1)
                act.wait_ge(kg16_ready, 1)
                for b in range(B):
                    nc.scalar.activation(xb[b // 2][:, b % 2, 0, :, 0:COL_V],
                                         kg16[:, b, 0, :].unsqueeze(1).to_broadcast([T, HEADS, COL_V]),
                                         ACT.Copy).then_inc(xg_hi, 1)
                for m in range(CC):
                    act.wait_ge(vt_ready, m + 1)
                    nc.scalar.activation(vT[:, m, :], ps_vt[m % 2][:, 0:B * T], ACT.Copy).then_inc(vt_read, 1)
                act.wait_ge(scaled, 1)
                act.wait_ge(v_ready, B)
                for b in range(B):
                    nc.scalar.activation(xb[b // 2][:, b % 2, 0, (CC - 1) * HG:HEADS, COL_V:XW],
                                         ps_Q[0:T, b * P:(b + 1) * P].rearrange("t (h d) -> t h d", d=DH),
                                         ACT.Copy, scale=ss[0:T, 10:11]).then_inc(xv_hi, 1)
                for b in range(B):
                    nc.scalar.activation(xb[b // 2][:, b % 2, 0, 0:(CC - 1) * HG, COL_V:XW],
                                         ps_v[b][0:T, 0:VC].rearrange("t (h d) -> t h d", d=DH),
                                         ACT.Copy, scale=ss[0:T, 10:11]).then_inc(xv_hi, 1)
                act.wait_ge(ld_b, 16)
                nc.scalar.activation(b_sp[0], b_raw, ACT.Copy).then_inc(b_hi, 1)
                for n in range(2 * CC):
                    c, h = divmod(n, 2)
                    act.wait_ge(vw_ready, n + 1)
                    nc.scalar.activation(vw[0][:, c, h * HALF:(h + 1) * HALF], ps_vw[n % 2][0:B * GI, 0:HALF],
                                         ACT.Copy).then_inc(vw_hi, 1)

            @block.vector
            def _(v):
                chain = [0]

                def link(ins):
                    chain[0] += 1
                    ins.then_inc(dve, 1)
                    v.wait_ge(dve, chain[0])

                nc.vector.memset(kg16[:, :, 1, :], 0.0).then_inc(dve, 1)
                nc.vector.memset(kg16[:, :, 0, T_ALL:T_ALL + 1], 1.0).then_inc(dve, 1)
                chain[0] += 2
                link(nc.vector.memset(amax[:], 0.0))
                for c in range(1, EC, 2):
                    v.wait_ge(tr_ready, c + 1)
                    nc.vector.tensor_copy(ctxT[:, c].rearrange("p b t -> p (b t)"),
                                          ps_S[1][:, 0:B * T_ALL]).then_inc(tr_odd, 1)
                v.wait_ge(tr_even, EC // 2)
                v.wait_ge(tr_odd, EC // 2)
                nc.vector.tensor_copy(ipT[:], ctxT[:, :, :, T:T_ALL]).then_inc(ip_ready, 1)
                v.wait_ge(sq_ready, 1)
                sq, y, t = ss[0:N16, 1:2], ss[0:N16, 2:3], ss[0:N16, 3:4]
                link(nc.vector.tensor_scalar(sq, ss[0:N16, 0:1], TINY, None, ALU.max))
                link(nc.vector.tensor_scalar(y.bitcast(I32), sq.bitcast(I32), -0.5, RSQRT_MAGIC, ALU.mult, ALU.add))
                for _ in range(4):
                    link(nc.vector.tensor_tensor(t, y, y, ALU.mult))
                    link(nc.vector.scalar_tensor_tensor(out=t, in0=t, scalar=-0.5, in1=sq, op0=ALU.mult, op1=ALU.mult))
                    link(nc.vector.scalar_tensor_tensor(out=y, in0=t, scalar=1.5, in1=y, op0=ALU.add, op1=ALU.mult))
                link(nc.vector.tensor_scalar(y, y, 1.0 / EPS, None, ALU.min))
                nc.vector.tensor_scalar(ipn[:], ipn[:], y, None, ALU.mult).then_inc(ipn_ready, 1)

                def key_lo(c):
                    v.wait_ge(k_hi, 2 * c + 2)
                    for s0, s1, t0, t1 in ((0, B * T, 0, T), (B * T, B * T_ALL, T, T_ALL)):
                        nc.vector.tensor_tensor(kt[1][:, c, :, t0:t1],
                                                ps_U[c % 2][:, s0:s1].rearrange("p (b t) -> p b t", b=B),
                                                kt[0][:, c, :, t0:t1].bitcast(F32), ALU.subtract).then_inc(k_lo, 1)

                key_lo(0)
                link(nc.vector.tensor_reduce(amax[0:T_ALL, 4:5], ctx_sb[:].rearrange("t b e -> t (b e)"), AX.X, ALU.max,
                                             apply_absolute_value=True))
                nc.vector.tensor_copy(amax[0:T_ALL, 0:1], amax[0:T_ALL, 4:5]).then_inc(local_max, 1)
                key_lo(1)
                v.wait_ge(wq_hi, 1)
                nc.vector.tensor_tensor(wq[1][:], w_raw[:], wq[0][:].bitcast(F32), ALU.subtract).then_inc(wq_lo, 1)
                for c in range(2, CC):
                    key_lo(c)
                v.wait_ge(ipt_ready, 1)
                v.wait_ge(ip_ready, 1)
                nc.vector.tensor_copy(ctxT[:, :, :, T:T_ALL],
                                      ps_M[:, 0:EC * N16].rearrange("p (c b n) -> p c b n", c=EC, b=B)).then_inc(ipt_read, 1)
                v.wait_ge(all_max, 1)
                link(nc.vector.tensor_scalar(ss[:, 4:5], amax[:, 2:3], 1e-30, None, ALU.max))
                link(nc.vector.tensor_scalar(ss[:, 4:5].bitcast(I32), ss[:, 4:5].bitcast(I32), 0x7F800000, None,
                                             ALU.bitwise_and))
                link(nc.vector.reciprocal(ss[:, 6:7], ss[:, 4:5]))
                link(nc.vector.tensor_scalar(ss[:, 8:9], ss[:, 6:7], ss[:, 6:7], K_SCALE, ALU.mult, ALU.mult))
                link(nc.vector.tensor_scalar(ss[:, 9:10], ss[:, 6:7], G_SCALE, None, ALU.mult))
                link(nc.vector.tensor_scalar(inv_eps, ss[:, 4:5], 1.0 / (EPS * G_SCALE), None, ALU.mult))
                for b in range(B):
                    v.wait_ge(kg_ready, b + 1)
                    nc.vector.tensor_copy(kg_raw[:, b, :], ps_S[b % 2][0:T, 0:T_ALL]).then_inc(kg_read, 1)
                v.wait_ge(kg_read, B)
                columns = ((0, T, ss[0:T, 8:9]), (T, T_ALL, ss[0:T, 9:10]))
                for c0, c1, sc in columns:
                    nc.vector.tensor_scalar(kg16[:, :, 0, c0:c1], kg_raw[:, :, c0:c1], sc, None,
                                            ALU.mult).then_inc(kg16_hi, 1)
                v.wait_ge(kg16_hi, 2)
                for c0, c1, sc in columns:
                    last = nc.vector.scalar_tensor_tensor(out=kg16[:, :, 1, c0:c1], in0=kg_raw[:, :, c0:c1],
                                                          scalar=sc, in1=kg16[:, :, 0, c0:c1],
                                                          op0=ALU.mult, op1=ALU.subtract)
                    link(last)
                nc.vector.memset(ss[:, 15:16], 0.0).then_inc(kg16_ready, 1)
                for b in range(B):
                    link(nc.vector.tensor_copy(xb[b // 2][:, b % 2, 1, :, 0:COL_V],
                                               kg16[:, b, 1, :].unsqueeze(1).to_broadcast([T, HEADS, COL_V])))
                v.wait_ge(wo_hi, 1)
                nc.vector.tensor_tensor(wo[1][:], w_raw[:], wo[0][:].bitcast(F32), ALU.subtract).then_inc(wo_lo, 1)
                for m in range(CC):
                    v.wait_ge(vt_read, m + 1)
                    nc.vector.tensor_reduce(amax[:, 8 + m:9 + m], vT[:, m, :], AX.X, ALU.max,
                                            apply_absolute_value=True).then_inc(vt_max, 1)
                v.wait_ge(vt_max, CC)
                nc.vector.tensor_reduce(amax[:, 1:2], amax[:, 8:8 + CC], AX.X, ALU.max).then_inc(local_max, 1)
                v.wait_ge(all_max, 2)
                link(nc.vector.tensor_scalar(ss[:, 5:6], amax[:, 3:4], 1e-30, None, ALU.max))
                link(nc.vector.tensor_scalar(ss[:, 5:6].bitcast(I32), ss[:, 5:6].bitcast(I32), 0x7F800000, None,
                                             ALU.bitwise_and))
                link(nc.vector.reciprocal(ss[:, 7:8], ss[:, 5:6]))
                nc.vector.tensor_scalar(ss[:, 10:11], ss[:, 7:8], float(2 ** 14), None, ALU.mult).then_inc(scaled, 1)
                link(nc.vector.tensor_scalar(inv_sv, ss[:, 5:6], float(2 ** -14), None, ALU.mult))
                v.wait_ge(scaled, 1)
                v.wait_ge(xv_hi, B)
                for b in range(B):
                    nc.vector.scalar_tensor_tensor(out=xb[b // 2][:, b % 2, 1, (CC - 1) * HG:HEADS, COL_V:XW],
                                                   in0=ps_Q[0:T, b * P:(b + 1) * P].rearrange("t (h d) -> t h d", d=DH),
                                                   scalar=ss[0:T, 10:11],
                                                   in1=xb[b // 2][:, b % 2, 0, (CC - 1) * HG:HEADS, COL_V:XW],
                                                   op0=ALU.mult, op1=ALU.subtract).then_inc(x_lo, 1)
                for b in range(B):
                    v.wait_ge(xv_hi, B + b + 1)
                    nc.vector.scalar_tensor_tensor(out=xb[b // 2][:, b % 2, 1, 0:(CC - 1) * HG, COL_V:XW],
                                                   in0=ps_v[b][0:T, 0:VC].rearrange("t (h d) -> t h d", d=DH),
                                                   scalar=ss[0:T, 10:11],
                                                   in1=xb[b // 2][:, b % 2, 0, 0:(CC - 1) * HG, COL_V:XW],
                                                   op0=ALU.mult, op1=ALU.subtract).then_inc(x_lo, 1)
                v.wait_ge(b_hi, 1)
                nc.vector.tensor_tensor(b_sp[1], b_raw, b_sp[0].bitcast(F32), ALU.subtract).then_inc(b_lo, 1)
                for h in range(2):
                    v.wait_ge(vip_ready, h + 1)
                    nc.vector.tensor_copy(vip_sb[:, h * HALF:(h + 1) * HALF], ps_U[h][0:N16, 0:HALF]).then_inc(vip_copied, 1)
                v.wait_ge(vipt_ready, 1)
                v.wait_ge(bd_zero, 1)
                for j in range(HG):
                    r = slice(j * DH, (j + 1) * DH)
                    nc.vector.tensor_copy(vip_bd[r, :, :, j, :],
                                          ps_S[0][r, 0:CC * N16].rearrange("p (c b n) -> p c b n", c=CC, b=B)
                                          ).then_inc(vip_read, 1)
                for n in range(2 * CC):
                    c, h = divmod(n, 2)
                    cols = slice(h * HALF, (h + 1) * HALF)
                    v.wait_ge(vw_hi, n + 1)
                    nc.vector.tensor_tensor(vw[1][:, c, cols], ps_vw[n % 2][0:B * GI, 0:HALF],
                                            vw[0][:, c, cols].bitcast(F32), ALU.subtract).then_inc(vw_lo, 1)

            @block.tensor
            def _(pe):
                pe.wait_ge(made_ident, 2)
                pe.wait_ge(ld_ctx, 16)
                for c in range(EC):
                    if c >= 2:
                        pe.wait_ge(tr_even if c % 2 == 0 else tr_odd, c // 2)
                    for b in range(B):
                        last = nc.tensor.transpose(ps_S[c % 2][:, b * T_ALL:(b + 1) * T_ALL],
                                                   ctx_sb[:, b, c * P:(c + 1) * P], ident[0:T_ALL, 0:T_ALL])
                    last.then_inc(tr_ready, 1)
                pe.wait_ge(tr_even, EC // 2)
                pe.wait_ge(tr_odd, EC // 2)
                pe.wait_ge(ip_ready, 1)
                for m in range(CC):
                    if m >= 2:
                        pe.wait_ge(k_lo, 2 * (m - 1))
                    for lo_c, hi_c, rows, w, ld in ((0, B * T, ctxT[:, :, :, 0:T], w_k, ld_wk),
                                                    (B * T, B * T_ALL, ipT[:], w_ip, ld_wkip)):
                        pe.wait_ge(ld, 16)
                        for c in range(EC):
                            last = nc.tensor.matmul(
                                ps_U[m % 2][:, lo_c:hi_c].rearrange("p (b t) -> p b t", b=B),
                                w[:, c, m * P:(m + 1) * P], rows[:, c], start=c == 0, stop=c == EC - 1)
                    last.then_inc(k_ready, 1)
                pe.wait_ge(ipn_ready, 1)
                for c in range(EC):
                    last = nc.tensor.transpose(ps_M[:, c * N16:(c + 1) * N16], ipn[:, c * P:(c + 1) * P],
                                               ident[0:N16, 0:N16])
                last.then_inc(ipt_ready, 1)
                pe.wait_ge(ipt_read, 1)
                for b in range(B):
                    if b >= 2:
                        pe.wait_ge(kg_read, b - 1)
                    for c in range(EC):
                        last = nc.tensor.matmul(ps_S[b % 2][0:T, 0:T_ALL], ctxT[:, c, b, 0:T], ctxT[:, c, b, :],
                                                start=c == 0, stop=c == EC - 1)
                    last.then_inc(kg_ready, 1)
                pe.wait_ge(ld_wv, 16)
                pe.wait_ge(k_lo, 2 * CC)
                for m in range(CC):
                    if m >= 2:
                        pe.wait_ge(vt_read, m - 1)
                    for c in range(EC):
                        last = nc.tensor.matmul(ps_vt[m % 2][:, 0:B * T].rearrange("p (b t) -> p b t", b=B),
                                                w_v[:, c, m * P:(m + 1) * P], ctxT[:, c, :, 0:T],
                                                start=c == 0, stop=c == EC - 1)
                    last.then_inc(vt_ready, 1)
                pe.wait_ge(kg_read, B)
                pe.wait_ge(vt_read, CC)
                for b in range(B):
                    for m in range(CC):
                        dst = ps_v[b][0:T, m * P:(m + 1) * P] if m < CC - 1 else ps_Q[0:T, b * P:(b + 1) * P]
                        last = nc.tensor.transpose(dst, vT[:, m, b * T:(b + 1) * T], ident[:])
                    last.then_inc(v_ready, 1)
                pe.wait_ge(ld_wvip, 16)
                for h in range(2):
                    for c in range(EC):
                        last = nc.tensor.matmul(ps_U[h][0:N16, 0:HALF], ipT[:, c].rearrange("p b n -> p (b n)"),
                                                w_ip[:, c, h * HALF:(h + 1) * HALF], start=c == 0, stop=c == EC - 1)
                    last.then_inc(vip_ready, 1)
                pe.wait_ge(vip_copied, 2)
                pe.wait_ge(x_lo, B + 1)
                for c in range(CC):
                    last = nc.tensor.transpose(ps_S[0][:, c * N16:(c + 1) * N16], vip_sb[:, c * P:(c + 1) * P],
                                               ident[0:N16, 0:N16])
                last.then_inc(vipt_ready, 1)
                pe.wait_ge(vip_read, HG)
                pe.wait_ge(ld_wo, 16)
                for n in range(2 * CC):
                    c, h = divmod(n, 2)
                    if n >= 2:
                        pe.wait_ge(vw_lo, n - 1)
                    last = nc.tensor.matmul(ps_vw[n % 2][0:B * GI, 0:HALF],
                                            vip_bd[:, c].rearrange("p b j n -> p (b j n)"),
                                            w_raw[:, c, h * HALF:(h + 1) * HALF], start=True, stop=True)
                    last.then_inc(vw_ready, 1)


class Window:

    def __init__(self, b, first=False, last=False):
        self.b, self.first, self.last = b, first, last

    def has(self, n):
        return not (self.first and n < 0) and not (self.last and n >= 0)

    def count(self, per_batch, n):
        return self.b * per_batch + n


def main_loop(nc, top, g):
    P, B, S, C, T, T_ALL, CC = (g[k] for k in "P B S C T T_ALL CC".split())
    XW, COL_G, COL_ONE, COL_V, IPR, HALF, DH, SPLIT = (
        g[k] for k in "XW COL_G COL_ONE COL_V IPR HALF DH SPLIT".split())
    NI, SLOTS, GK, SCALE = (g[k] for k in "NI SLOTS GK SCALE".split())
    ps_S, ps_U, ps_Q, ps_M, ps_O, ps_PT = (g[k] for k in "ps_S ps_U ps_Q ps_M ps_O ps_PT".split())
    ident, ident16, wq, wo, mask_sb, inv_sv, inv_eps = (
        g[k] for k in "ident ident16 wq wo mask_sb inv_sv inv_eps".split())
    kt_d, x_d, vw_d, x, out = (g[k] for k in "kt_d x_d vw_d x out".split())
    UNITS = SLOTS * SUB
    OUTS = 2 * SUB
    AT_RING, P_RING, SIP_RING = 2 * CC, 4, 4
    X_RING = NI
    assert NI == 4 and SLOTS % 4 == 0 and SLOTS % AT_RING == 0
    LT, LU = 2, 3
    PASSES = ((0, 0), (0, 1), (1, 0))
    STACK = (P, 2 * T - SPLIT)
    LO_B, HI, LO_A = 0, T - SPLIT, 2 * T - SPLIT
    Q_MMS = [(c, a, m) for c in range(CC) for a, m in PASSES]
    O_MMS = [(k, a, m) for k in range(CC + 1) for a, m in PASSES]
    Q_PARTS = 3
    Q_PIECE, O_PIECE = len(Q_MMS) // Q_PARTS, len(O_MMS) // 2

    def sb(name, shape, dt):
        return top.enter_context(nc.sbuf_tensor(name, shape, dt))

    def sem(name):
        return top.enter_context(nc.semaphore(name))

    kbd = sb("kbd", [P, 2, CC, GK], F32R)
    xm = sb("xm", [P, 2, HEADS, XW], F16)
    vw = sb("vw_sb", [IPR + 1, 2, C], F32R)
    x_in = [g["x_in0"]] + [sb(f"x_in{i}", [P, SUB, C], F32) for i in range(1, X_RING)]
    xT = [sb("xT_hi", [P, CC, TILE], F32R), sb("xT_lo", [P, CC, TILE], F32R)]
    qT = [[sb(f"qT{r}_{k}", [P, TILE], F32R) for k in range(2)] for r in range(2)]
    smax = [sb(f"smax{i}", [P, HG], F32) for i in range(2)]
    bias = [sb(f"bias{i}", [P, HG], F32) for i in range(2)]
    s_ip = [sb(f"s_ip{i}", [P, SUB * HG, N_IP], F32) for i in range(SIP_RING)]
    pr = [sb(f"pr{i}", [P, HG, T], F32) for i in range(P_RING)]
    ph = [sb(f"ph{i}", [P, HG, 2 * T], F16) for i in range(2)]
    pts = [sb(f"pts{i}", [P, HG, 2, P], F16) for i in range(2)]
    n2 = [sb(f"n2_{i}", [P, SUB * HG], F32) for i in range(2)]
    nd = [sb(f"nd{i}", [P, SUB * HG, N_IP + 1], F32) for i in range(2)]
    rd = [sb(f"rd{i}", [P, SUB * HG], F32) for i in range(2)]
    attn = [sb(f"attn{i}", [P, SUB, HG, DH], F32) for i in range(2)]
    aT = [[sb(f"aT{r}_{k}", [P, TILE], F32R) for k in range(2)] for r in range(AT_RING)]
    pip = sb("pip", [P, SUB, IPR + 1], F32)
    pipT = [sb(f"pipT{k}", [IPR + 1, TILE], F32R) for k in range(2)]
    NH = SUB * HG
    n2h, y, yt, rde, w_sem, fmx, se, three_halves = (
        sb(n, [P, NH], F32) for n in "n2h y yt rde w_sem fmx se three_halves".split())
    f = sb("f", [P, NH, N_IP], F32)
    ef = sb("ef", [P, NH, N_IP], F32)

    x_loaded = [g["x_loaded0"]] + [sem(f"x_loaded{i}") for i in range(1, X_RING)]
    x_stored = [sem(f"x_stored{i}") for i in range(X_RING)]
    kbd_loaded = [sem(f"kbd_loaded{k}") for k in range(CC)]
    xm_loaded = [sem(f"xm_loaded{k}") for k in range(CC)]
    vw_loaded, cleared = sem("vw_loaded"), sem("cleared")
    xT_ready, xT_hi, xT_lo = sem("xT_ready"), sem("xT_hi_done"), sem("xT_lo_done")
    q_ready, q_hi, q_lo = sem("q_ready"), sem("q_hi_done"), sem("q_lo_done")
    s_ready, max_done, s_read, bias_ready = sem("s_ready"), sem("max_done"), sem("s_read"), sem("bias_ready")
    p_ready, ph_ready, pl_ready = sem("p_ready"), sem("ph_ready"), sem("pl_ready")
    pt_ready, pts_ready = sem("pt_ready"), sem("pts_ready")
    u_ready, nd_done, prod_done, rd_done, n2_done, attn_ready = (
        sem(n) for n in "u_ready nd_done prod_done rd_done n2_done attn_ready".split())
    aT_ready, aT_hi, aT_lo = sem("aT_ready"), sem("aT_hi_done"), sem("aT_lo_done")
    n2h_done, y0_ready, newton_step, y_ready = (sem(n) for n in "n2h_done y0_ready newton_step y_ready".split())
    rde_done, f_step, f_ready, ef_ready, se_done, rs_ready, mask_done, pip_ready = (
        sem(n) for n in "rde_done f_step f_ready ef_ready se_done rs_ready mask_done pip_ready".split())
    pT_ready, pT_hi, pT_lo = sem("pT_ready"), sem("pT_hi_done"), sem("pT_lo_done")
    o_ready, o_added = sem("o_ready"), sem("o_added")
    bank = {"M": ps_M, "Q": ps_Q, "O": ps_O}

    Q_AT = {(4, 0): (1, 0), (4, 1): (1, 1), (4, 2): (1, 2), (4, 3): (2, 0), (0, 0): (1, 1), (0, 1): (1, 2),
            (0, 2): (2, 0), (0, 3): (2, 1), (1, 0): (1, 2), (1, 2): (2, 0), (1, 3): (2, 1), (2, 0): (1, 2),
            (2, 2): (2, 0), (2, 3): (2, 1), (3, 0): (1, 2)}
    OUT_AT = {(6, 3): (0, 0), (7, 0): (0, 1), (7, 1): (1, 0), (7, 2): (1, 1), (8, 0): (2, 0), (8, 1): (2, 1),
              (8, 2): (3, 0), (8, 3): (3, 1), (9, 0): (4, 0), (9, 2): (4, 1), (9, 3): (5, 0), (10, 0): (5, 1),
              (10, 2): (6, 0), (10, 3): (6, 1), (11, 0): (7, 0), (11, 1): (7, 1)}
    STORE_AT = {(7, 3): 0, (9, 0): 1, (10, 1): 2, (11, 2): 3}
    XT_AT = {(2, 3): (0, "M"), (3, 0): (1, "M"), (3, 1): (2, "Q"), (3, 2): (3, "M"), (3, 3): (4, "Q")}
    FIRST, LAST, TAIL = -4, SLOTS - 4, 7

    def extras(w, slot, s):
        todo = []
        i, k = divmod(slot, CC)
        if (k, s) in Q_AT:
            ahead, part = Q_AT[k, s]
            if w.has(slot + ahead):
                todo.append(("q", slot + ahead, 0, part, "Q"))
        for back in range(3):
            if w.has(i - back) and (k + CC * back, s) in OUT_AT:
                half, part = OUT_AT[k + CC * back, s]
                entry = ("out", i - back, half, part, "Q" if w.last and i - back == -1 and half % 2 else "O")
                todo.insert(len(todo) - 1 if todo and todo[-1][0] == "q" and todo[-1][3] < 2 else len(todo), entry)
        if s == 1 and w.has(slot - 2):
            todo.append(("attn", slot - 2, 0, 0, "M"))
        if (k, s) in XT_AT and w.has(i + 1):
            c, m = XT_AT[k, s]
            todo.append(("x", i + 1, c, 0, "MOQMO"[c] if w.first and i + 1 == 0 else m))
        if k == 1 and s == 2 and w.has(i - 1):
            todo.append(("ip", i - 1, 0, 0, "M"))
        return todo

    def before(slot, s):
        return (slot, s - 1) if s else (slot - 1, SUB - 1)

    def finished(w, slot, s):
        last_part = {"q": Q_PARTS - 1, "out": 1}
        done = [e for e in extras(w, *before(slot, s)) if e[3] == last_part.get(e[0], 0)]
        return sorted(done, key=lambda e: ("out", "q").index(e[0]) if e[0] in ("out", "q") else 2)

    def emptied(w, kind, i, c):
        return {"x": (xT_lo, w.count(SLOTS, CC * i + c + 1)), "q": (q_lo, w.count(SLOTS, i + 1)),
                "attn": (aT_lo, w.count(SLOTS, i + 1)), "ip": (pT_lo, w.count(NI, i + 1)),
                "out": (o_added, w.count(NI * OUTS, OUTS * i + c + 1))}[kind]

    def user_before(w, slot, s, entry):
        at = extras(w, slot, s)
        at = at[:at.index(entry)]
        for _ in range(UNITS):
            for e in reversed(at):
                if e[4] == entry[4]:
                    return e
            slot, s = before(slot, s)
            at = extras(w, slot, s)
        return None

    def steps(w):
        for slot in range(FIRST, TAIL if w.last else LAST):
            for s in range(SUB):
                yield SUB * slot + s, slot, s

    with nc.Block() as block:
        @block.sync
        def _(sp):
            def turn(w):
                def rows(dram, i):
                    return dram[bass.ds(w.b + i // NI, 1)].rearrange("a (i s p) c -> (a i) p s c", s=SUB, p=P)[i % NI]

                for t, slot, s in steps(w):
                    i, k = divmod(slot, CC)
                    if s == 0 and k == 1 and w.has(i + 1) and not (w.first and i + 1 == 0):
                        if w.has(i + 1 - X_RING):
                            sp.wait_ge(x_stored[(i + 1) % X_RING], w.count(16 * SUB, 0))
                        sp.dma_start(x_in[(i + 1) % X_RING][:], rows(x, i + 1)).then_inc(x_loaded[(i + 1) % X_RING], 16)
                    if s == 0 and FIRST <= slot < FIRST + CC and not w.last:
                        kg = slot - FIRST
                        if w.first and kg == 0:
                            sp.wait_ge(cleared, 3)
                        if w.has(SUB * slot - 1):
                            sp.wait_ge(s_ready, w.count(UNITS, SUB * slot))
                        for j in range(HG):
                            r = slice(j * DH, (j + 1) * DH)
                            sp.dma_start(kbd[r, :, kg, j * T_ALL:(j + 1) * T_ALL].bitcast(F32),
                                         kt_d[bass.ds(w.b, 1)].rearrange("a c k p t -> (a c) p k t")[kg, r]
                                         ).then_inc(kbd_loaded[kg], 16)
                    if s == 0 and FIRST < slot <= FIRST + CC and not w.last:
                        kg = slot - FIRST - 1
                        if w.has(SUB * (slot - 1) - 1):
                            sp.wait_ge(u_ready, w.count(UNITS, SUB * (slot - 1)))
                        for tile, rows_used in enumerate(STACK):
                            sp.dma_start(xm[0:rows_used, tile, kg * HG:(kg + 1) * HG, :],
                                         x_d[bass.ds(w.b, 1)].rearrange("a k p h w -> (a k) p h w")
                                         [tile, 0:rows_used, kg * HG:(kg + 1) * HG, :]).then_inc(xm_loaded[kg], 16)
                    if s == 2 and slot == 6 and not w.last:
                        if w.has(-1):
                            sp.wait_ge(o_ready, w.count(NI * OUTS, 0))
                        sp.dma_start(vw[:].bitcast(F32),
                                     vw_d[bass.ds(w.b, 1)].rearrange("a r k c -> (a r) k c")).then_inc(vw_loaded, 16)
                    for back in (1, 2):
                        if w.has(i - back) and (k + CC * back, s) in STORE_AT:
                            j, q = i - back, STORE_AT[k + CC * back, s]
                            sp.wait_ge(o_added, w.count(NI * OUTS, OUTS * j + 2 * q + 2))
                            sp.dma_start(rows(out, j)[:, q], x_in[j % X_RING][:, q, :]).then_inc(x_stored[j % X_RING], 16)

            turn(Window(0, first=True))
            with sp.Fori(1, B) as b:
                turn(Window(b))
            turn(Window(B, last=True))
            for r in range(X_RING):
                sp.wait_ge(x_stored[r], 16 * SUB * B)

        @block.scalar
        def _(act):
            def turn(w):
                for t, slot, s in steps(w):
                    u = t - 1
                    if w.has(u):
                        act.wait_ge(p_ready, w.count(UNITS, u + 1))
                        if w.has(u - 2):
                            act.wait_ge(pt_ready, w.count(UNITS, u - 1))
                            act.wait_ge(pl_ready, w.count(2 * UNITS, 2 * (u - 1)))
                        nc.scalar.activation(ph[u % 2][:, :, HI:LO_A], pr[u % P_RING][:], ACT.Copy).then_inc(ph_ready, 1)
                    for kind, i, c, _, m in finished(w, slot, s):
                        if kind == "x":
                            act.wait_ge(xT_ready, w.count(SLOTS, CC * i + c + 1))
                            if w.has(i - 1):
                                part = Q_MMS.index((c, *PASSES[-1])) // Q_PIECE
                                act.wait_ge(q_ready, w.count(Q_PARTS * SLOTS, Q_PARTS * (CC * i - 1) + part + 1))
                            nc.scalar.activation(xT[0][:, c, :], bank[m][:], ACT.Copy).then_inc(xT_hi, 1)
                        elif kind == "q":
                            act.wait_ge(q_ready, w.count(Q_PARTS * SLOTS, Q_PARTS * (i + 1)))
                            if w.has(i - 2):
                                act.wait_ge(s_ready, w.count(UNITS, SUB * (i - 1)))
                            nc.scalar.activation(qT[i % 2][0][:], ps_Q[:], ACT.Copy).then_inc(q_hi, 1)
                        elif kind == "attn":
                            act.wait_ge(aT_ready, w.count(SLOTS, i + 1))
                            if w.has(i - AT_RING):
                                act.wait_ge(o_ready, w.count(NI * OUTS, OUTS * ((i - AT_RING) // CC + 1)))
                            nc.scalar.activation(aT[i % AT_RING][0][:], ps_M[:], ACT.Copy, scale=inv_sv).then_inc(aT_hi, 1)
                        elif kind == "ip":
                            act.wait_ge(pT_ready, w.count(NI, i + 1))
                            if w.has(i - 1):
                                act.wait_ge(o_ready, w.count(NI * OUTS, OUTS * i))
                            nc.scalar.activation(pipT[0][:], ps_M[0:IPR + 1, :], ACT.Copy).then_inc(pT_hi, 1)
                    n = slot - 2
                    if s == 1 and w.has(n):
                        act.wait_ge(f_ready, w.count(SLOTS, n + 1))
                        if w.has(n - 1):
                            act.wait_ge(pip_ready, w.count(SLOTS, n))
                        nc.scalar.activation(ef[:], f[:], ACT.Exp, scale=SCALE).then_inc(ef_ready, 1)
                    u = t - LT
                    if w.has(u):
                        act.wait_ge(pt_ready, w.count(UNITS, u + 1))
                        if w.has(u - 2):
                            act.wait_ge(u_ready, w.count(UNITS, u - 1))
                        nc.scalar.activation(pts[u % 2][:].rearrange("t h k p -> t (h k p)"), ps_PT[:],
                                             ACT.Copy).then_inc(pts_ready, 1)
                    if w.has(t):
                        sc = ps_S[t % 2][:, 0:GK].rearrange("p (h t) -> p h t", h=HG)
                        act.wait_ge(bias_ready, w.count(UNITS, t + 1))
                        if w.has(t - P_RING):
                            act.wait_ge(n2_done, w.count(UNITS, t - P_RING + 1))
                        for h in range(HG):
                            last = nc.scalar.activation(pr[t % P_RING][:, h, :], sc[:, h, 0:T], ACT.Exp,
                                                        bias=bias[t % 2][:, h:h + 1], scale=SCALE)
                        last.then_inc(p_ready, 1)

            turn(Window(0, first=True))
            with act.Fori(1, B) as b:
                turn(Window(b))
            turn(Window(B, last=True))

        @block.gpsimd
        def _(pool):
            nc.gpsimd.memset(kbd[:].bitcast(F32), 0.0).then_inc(cleared, 1)
            nc.gpsimd.memset(pip[:, :, IPR:IPR + 1], 1.0).then_inc(cleared, 1)
            nc.gpsimd.memset(three_halves[:], 1.5).then_inc(cleared, 1)
            pool.wait_ge(cleared, 3)
            NEWTON = 3
            LINKS = 4 * NEWTON - 1

            def turn(w):
                for t, slot, s in steps(w):
                    u = t - 1
                    if w.has(u):
                        pool.wait_ge(ph_ready, w.count(UNITS, u + 1))
                        if w.has(u - 2):
                            pool.wait_ge(pt_ready, w.count(UNITS, u - 1))
                        for col, t0, t1 in ((LO_A, 0, SPLIT), (LO_B, SPLIT, T)):
                            nc.gpsimd.tensor_tensor(ph[u % 2][:, :, col:col + t1 - t0], pr[u % P_RING][:, :, t0:t1],
                                                    ph[u % 2][:, :, HI + t0:HI + t1], ALU.subtract).then_inc(pl_ready, 1)
                    n = slot - 1
                    if s == 3 and w.has(n):
                        pool.wait_ge(y0_ready, w.count(SLOTS, n + 1))
                        link = LINKS * n
                        for it in range(NEWTON):
                            nc.gpsimd.tensor_tensor(yt[:], y[:], y[:], ALU.mult).then_inc(newton_step, 1)
                            pool.wait_ge(newton_step, w.count(LINKS * SLOTS, link + 1))
                            nc.gpsimd.tensor_tensor(yt[:], yt[:], n2h[:], ALU.mult).then_inc(newton_step, 1)
                            pool.wait_ge(newton_step, w.count(LINKS * SLOTS, link + 2))
                            nc.gpsimd.tensor_tensor(yt[:], three_halves[:], yt[:], ALU.subtract).then_inc(newton_step, 1)
                            pool.wait_ge(newton_step, w.count(LINKS * SLOTS, link + 3))
                            step = nc.gpsimd.tensor_tensor(y[:], y[:], yt[:], ALU.mult)
                            if it < NEWTON - 1:
                                step.then_inc(newton_step, 1)
                                pool.wait_ge(newton_step, w.count(LINKS * SLOTS, link + 4))
                            else:
                                step.then_inc(y_ready, 1)
                            link += 4
                    n = slot - 2
                    if s == 1 and w.has(n):
                        i, k = divmod(n, CC)
                        pool.wait_ge(rs_ready, w.count(SLOTS, n + 1))
                        j = i % NI
                        nc.gpsimd.tensor_tensor(
                            se[:].rearrange("p (s h) -> p s h", s=SUB), se[:].rearrange("p (s h) -> p s h", s=SUB),
                            mask_sb[:, j * SUB:(j + 1) * SUB].unsqueeze(2).to_broadcast([P, SUB, HG]),
                            ALU.mult).then_inc(mask_done, 1)
                        pool.wait_ge(mask_done, w.count(SLOTS, n + 1))
                        if k == 0 and w.has(i - 1):
                            pool.wait_ge(pT_ready, w.count(NI, i))
                        nc.gpsimd.tensor_tensor(
                            pip[:, :, k * HG * N_IP:(k + 1) * HG * N_IP].rearrange("p s (h n) -> p s h n", n=N_IP),
                            ef[:].rearrange("p (s h) n -> p s h n", s=SUB),
                            se[:].rearrange("p (s h) -> p s h", s=SUB).unsqueeze(3).to_broadcast([P, SUB, HG, N_IP]),
                            ALU.mult).then_inc(pip_ready, 1)

            turn(Window(0, first=True))
            with pool.Fori(1, B) as b:
                turn(Window(b))
            turn(Window(B, last=True))

        @block.vector
        def _(v):
            def lo_part(dst, src, hi, hi_done, n, signal):
                v.wait_ge(hi_done, n)
                nc.vector.tensor_tensor(dst, src, hi.bitcast(F32), ALU.subtract).then_inc(signal, 1)

            def turn(w):
                def f_link(n, k):
                    v.wait_ge(f_step, w.count(4 * SLOTS, 4 * n + k))

                for t, slot, s in steps(w):
                    for kind, i, c, _, m in finished(w, slot, s):
                        if kind == "out":
                            v.wait_ge(o_ready, w.count(NI * OUTS, OUTS * i + c + 1))
                            half = x_in[i % X_RING][:, c // 2, (c % 2) * HALF:(c % 2 + 1) * HALF]
                            nc.vector.tensor_tensor(half, bank[m][:, 0:HALF], half, ALU.add).then_inc(o_added, 1)
                        elif kind == "q":
                            lo_part(qT[i % 2][1][:], ps_Q[:], qT[i % 2][0][:], q_hi, w.count(SLOTS, i + 1), q_lo)
                    if w.has(t):
                        sc = ps_S[t % 2][:, 0:GK].rearrange("p (h t) -> p h t", h=HG)
                        v.wait_ge(s_ready, w.count(UNITS, t + 1))
                        if w.has(t - 2):
                            v.wait_ge(bias_ready, w.count(UNITS, t - 1))
                        nc.vector.tensor_reduce(smax[t % 2][:], sc[:, :, 0:T], AX.X, ALU.max).then_inc(max_done, 1)
                        if s == 0 and w.has(slot - SIP_RING):
                            v.wait_ge(f_ready, w.count(SLOTS, slot - SIP_RING + 1))
                        nc.vector.tensor_copy(s_ip[slot % SIP_RING][:, s * HG:(s + 1) * HG, :],
                                              sc[:, :, T:T_ALL]).then_inc(s_read, 1)
                        v.wait_ge(max_done, w.count(UNITS, t + 1))
                        if w.has(t - 2):
                            v.wait_ge(p_ready, w.count(UNITS, t - 1))
                        nc.vector.tensor_scalar(bias[t % 2][:], smax[t % 2][:], -SCALE, LN_PSCALE,
                                                ALU.mult, ALU.add).then_inc(bias_ready, 1)
                    for kind, i, c, _, m in finished(w, slot, s):
                        if kind == "x":
                            lo_part(xT[1][:, c, :], bank[m][:], xT[0][:, c, :], xT_hi, w.count(SLOTS, CC * i + c + 1), xT_lo)
                        elif kind == "attn":
                            v.wait_ge(aT_hi, w.count(SLOTS, i + 1))
                            nc.vector.scalar_tensor_tensor(out=aT[i % AT_RING][1][:], in0=ps_M[:], scalar=inv_sv,
                                                           in1=aT[i % AT_RING][0][:].bitcast(F32),
                                                           op0=ALU.mult, op1=ALU.subtract).then_inc(aT_lo, 1)
                        elif kind == "ip":
                            lo_part(pipT[1][:], ps_M[0:IPR + 1, :], pipT[0][:], pT_hi, w.count(NI, i + 1), pT_lo)
                    m = slot - 2
                    logits = w.has(m)
                    if s == 1 and logits:
                        v.wait_ge(ef_ready, w.count(SLOTS, m + 1))
                        if w.has(m - 1):
                            v.wait_ge(pip_ready, w.count(SLOTS, m))
                        nc.vector.tensor_reduce(se[:], ef[:], AX.X, ALU.add).then_inc(se_done, 1)
                    u = t - LU
                    un, us = divmod(u, SUB)
                    hs = slice(us * HG, (us + 1) * HG)
                    uo = ps_U[u % 2][:, 0:HG * XW].rearrange("p (h w) -> p h w", h=HG)
                    if w.has(u):
                        v.wait_ge(u_ready, w.count(UNITS, u + 1))
                        nc.vector.tensor_copy(nd[un % 2][:, hs, :], uo[:, :, COL_G:COL_V]).then_inc(nd_done, 1)
                    if s == 1 and logits:
                        v.wait_ge(se_done, w.count(SLOTS, m + 1))
                        nc.vector.reciprocal(se[:], se[:]).then_inc(rs_ready, 1)
                    if s == 0 and logits:
                        v.wait_ge(y_ready, w.count(SLOTS, m + 1))
                        if w.has(m - 1):
                            v.wait_ge(ef_ready, w.count(SLOTS, m))
                        v.wait_ge(rde_done, w.count(SLOTS, m + 1))
                        nc.vector.scalar_tensor_tensor(out=w_sem[:], in0=y[:], scalar=K_SCALE ** 0.5 / G_SCALE,
                                                       in1=rde[:], op0=ALU.mult, op1=ALU.min).then_inc(f_step, 1)
                    if w.has(u):
                        v.wait_ge(pl_ready, w.count(2 * UNITS, 2 * (u + 1)))
                        nc.vector.tensor_tensor(pr[u % P_RING][:], uo[:, :, 0:T], pr[u % P_RING][:],
                                                ALU.mult).then_inc(prod_done, 1)
                        v.wait_ge(nd_done, w.count(UNITS, u + 1))
                        nc.vector.reciprocal(rd[un % 2][:, hs], nd[un % 2][:, hs, N_IP]).then_inc(rd_done, 1)
                    if s == 0 and logits:
                        f_link(m, 1)
                        nc.vector.tensor_tensor(f[:], nd[m % 2][:, :, 0:N_IP],
                                                w_sem[:].unsqueeze(2).to_broadcast([P, NH, N_IP]),
                                                ALU.mult).then_inc(f_step, 1)
                    if w.has(u):
                        v.wait_ge(prod_done, w.count(UNITS, u + 1))
                        nc.vector.tensor_reduce(n2[un % 2][:, hs], pr[u % P_RING][:], AX.X, ALU.add).then_inc(n2_done, 1)
                    if s == 0 and logits:
                        f_link(m, 2)
                        nc.vector.scalar_tensor_tensor(out=f[:], in0=f[:], scalar=SEM_SCALE / SCALE,
                                                       in1=s_ip[m % SIP_RING][:], op0=ALU.mult, op1=ALU.add).then_inc(f_step, 1)
                    if w.has(u):
                        v.wait_ge(rd_done, w.count(UNITS, u + 1))
                        if w.has(un - 2) and us == 0:
                            v.wait_ge(aT_ready, w.count(SLOTS, un - 1))
                        nc.vector.tensor_tensor(attn[un % 2][:, us], uo[:, :, COL_V:XW],
                                                rd[un % 2][:, hs].unsqueeze(2).to_broadcast([P, HG, DH]),
                                                ALU.mult).then_inc(attn_ready, 1)
                    if s == 0 and logits:
                        f_link(m, 3)
                        nc.vector.tensor_reduce(fmx[:], f[:], AX.X, ALU.max).then_inc(f_step, 1)
                        f_link(m, 4)
                        nc.vector.tensor_tensor(f[:], f[:], fmx[:].unsqueeze(2).to_broadcast([P, NH, N_IP]),
                                                ALU.subtract).then_inc(f_ready, 1)
                    n = slot - 1
                    if s == 2 and w.has(n):
                        v.wait_ge(n2_done, w.count(UNITS, SUB * (n + 1)))
                        if w.has(n - 1):
                            v.wait_ge(f_ready, w.count(SLOTS, n))
                        nc.vector.tensor_scalar(n2h[:], n2[n % 2][:], TINY, 0.5, ALU.max, ALU.mult).then_inc(n2h_done, 1)
                        v.wait_ge(rd_done, w.count(UNITS, SUB * (n + 1)))
                        nc.vector.tensor_scalar(rde[:], rd[n % 2][:], inv_eps, None, ALU.mult).then_inc(rde_done, 1)
                        v.wait_ge(n2h_done, w.count(SLOTS, n + 1))
                        nc.vector.tensor_scalar(y[:].bitcast(I32), n2h[:].bitcast(I32), -0.5, RSQRT_MAGIC - 2 ** 22,
                                                ALU.mult, ALU.add).then_inc(y0_ready, 1)

            turn(Window(0, first=True))
            with v.Fori(1, B) as b:
                turn(Window(b))
            turn(Window(B, last=True))

        @block.tensor
        def _(pe):
            def turn(w):
                for t, slot, s in steps(w):
                    if w.has(t):
                        if s == 0:
                            pe.wait_ge(q_lo, w.count(SLOTS, slot + 1))
                            if 0 <= slot < CC:
                                pe.wait_ge(kbd_loaded[slot], w.count(16 * HG, 16 * HG))
                        if w.has(t - 2):
                            pe.wait_ge(s_read, w.count(UNITS, t - 1))
                            pe.wait_ge(p_ready, w.count(UNITS, t - 1))
                        for a, m in PASSES:
                            last = nc.tensor.matmul(ps_S[t % 2][:, 0:GK], qT[slot % 2][a][:, s * P:(s + 1) * P],
                                                    kbd[:, m, slot % CC, :], start=(a, m) == PASSES[0],
                                                    stop=(a, m) == PASSES[-1])
                        last.then_inc(s_ready, 1)
                    u = t - LT
                    if w.has(u):
                        pe.wait_ge(ph_ready, w.count(UNITS, u + 1))
                        pe.wait_ge(pl_ready, w.count(2 * UNITS, 2 * (u + 1)))
                        if w.has(u - 1):
                            pe.wait_ge(pts_ready, w.count(UNITS, u))
                        for h in range(HG):
                            for tile, col in ((1, LO_B), (0, HI)):
                                k = 2 * h + tile
                                last = nc.tensor.transpose(ps_PT[:, k * P:(k + 1) * P], ph[u % 2][:, h, col:col + P],
                                                           ident16[:])
                        last.then_inc(pt_ready, 1)
                    u = t - LU
                    if w.has(u):
                        un, us = divmod(u, SUB)
                        k0 = un % CC
                        if us == 0 and 0 <= un % SLOTS < CC:
                            pe.wait_ge(xm_loaded[k0], w.count(32, 32 * (un // SLOTS + 1)))
                        pe.wait_ge(pts_ready, w.count(UNITS, u + 1))
                        if w.has(u - 2):
                            pe.wait_ge(attn_ready, w.count(UNITS, u - 1))
                        for h in range(HG):
                            for tile, n in enumerate(STACK):
                                last = nc.tensor.matmul(ps_U[u % 2][:, h * XW:(h + 1) * XW], pts[u % 2][0:n, h, tile, :],
                                                        xm[0:n, tile, k0 * HG + h, :], start=tile == 0, stop=tile == 1)
                        last.then_inc(u_ready, 1)
                    for entry in extras(w, slot, s):
                        kind, i, c, part, m = entry
                        if part == 0:
                            was = user_before(w, slot, s, entry)
                            if was is not None:
                                pe.wait_ge(*emptied(w, *was[:3]))
                        if kind == "x":
                            if c == 0:
                                pe.wait_ge(x_loaded[i % X_RING], w.count(16, 16 * (i // NI + 1)))
                            for q in range(SUB):
                                last = nc.tensor.transpose(bank[m][:, q * P:(q + 1) * P],
                                                           x_in[i % X_RING][:, q, c * P:(c + 1) * P], ident[:])
                            last.then_inc(xT_ready, 1)
                        elif kind == "q":
                            ii, k = divmod(i, CC)
                            mms = Q_MMS[part * Q_PIECE:(part + 1) * Q_PIECE]
                            if k == 0:
                                pe.wait_ge(xT_lo, w.count(SLOTS, CC * ii + mms[-1][0] + 1))
                            for cc, a, b_ in mms:
                                last = nc.tensor.matmul(ps_Q[:], wq[a][:, cc, k * P:(k + 1) * P], xT[b_][:, cc, :],
                                                        start=(cc, a, b_) == Q_MMS[0], stop=(cc, a, b_) == Q_MMS[-1])
                            last.then_inc(q_ready, 1)
                        elif kind == "attn":
                            pe.wait_ge(attn_ready, w.count(UNITS, SUB * (i + 1)))
                            for q in range(SUB):
                                last = nc.tensor.transpose(ps_M[:, q * P:(q + 1) * P],
                                                           attn[i % 2][:, q].rearrange("p h d -> p (h d)"), ident[:])
                            last.then_inc(aT_ready, 1)
                        elif kind == "ip":
                            pe.wait_ge(pip_ready, w.count(SLOTS, CC * (i + 1)))
                            if w.first and i == 0:
                                pe.wait_ge(cleared, 3)
                            for q in range(SUB):
                                last = nc.tensor.transpose(ps_M[0:IPR + 1, q * P:(q + 1) * P], pip[:, q, :], ident[:])
                            last.then_inc(pT_ready, 1)
                        elif kind == "out":
                            q, h = divmod(c, 2)
                            cols = slice(h * HALF, (h + 1) * HALF)
                            if part == 0:
                                pe.wait_ge(aT_lo, w.count(SLOTS, CC * (i + 1)))
                            else:
                                pe.wait_ge(pT_lo, w.count(NI, i + 1))
                                if c == 0 and i % NI == 0:
                                    pe.wait_ge(vw_loaded, w.count(16, 16 * (i // NI + 1)))
                            for k, a, b_ in O_MMS[part * O_PIECE:(part + 1) * O_PIECE]:
                                if k < CC:
                                    stationary, moving = aT[(CC * i + k) % AT_RING][a], wo[b_][:, k, cols]
                                else:
                                    stationary, moving = pipT[a], vw[:, b_, cols]
                                last = nc.tensor.matmul(bank[m][:, 0:HALF], stationary[:, q * P:(q + 1) * P], moving,
                                                        start=(k, a, b_) == O_MMS[0], stop=(k, a, b_) == O_MMS[-1])
                            if part == 1:
                                last.then_inc(o_ready, 1)

            turn(Window(0, first=True))
            with pe.Fori(1, B) as b:
                turn(Window(b))
            turn(Window(B, last=True))


_INS = ["x", "ctx_2048", "fside_S_0", "L0_xattn_W_q", "L0_xattn_W_k", "L0_xattn_W_v", "L0_xattn_W_k_ip",
        "L0_xattn_W_v_ip", "L0_xattn_W_out", "L0_xattn_b_out"]


def kernel(**inputs):
    import numpy as _np
    import concourse.bacc as _bacc
    from concourse import mybir as _mybir
    from concourse.bass_utils import run_bass_kernel_spmd as _run

    nc = _bacc.Bacc("TRN2", target_bir_lowering=False, num_devices=1)
    arrays, args = {}, []
    for name in _INS:
        a = _np.ascontiguousarray(inputs[name])
        arrays[f"in_{name}_dram"] = a
        args.append(nc.dram_tensor(f"in_{name}_dram", a.shape, _mybir.dt.from_np(a.dtype), kind="ExternalInput").ap())
    args.append(nc.dram_tensor("out_0_dram", inputs["x"].shape, _mybir.dt.float32, kind="ExternalOutput").ap())
    xattn_kernel(nc, *args)
    r = _run(nc, [arrays], core_ids=[0])
    return r.results[0]["out_0_dram"]
```
